# Optimizing a Trainium2 kernel written in Bass

```python
import numpy as np
import jax
import jax.numpy as jnp

def _softmax(x, axis=-1):
    return jax.nn.softmax(x, axis=axis)

def _gelu(x):
    return jax.nn.gelu(x, approximate=True)

def _silu(x):
    return jax.nn.silu(x)

def _sigmoid(x):
    return jax.nn.sigmoid(x)

def _layernorm(x, axis=-1, eps=1e-05):
    m = jnp.mean(x, axis=axis, keepdims=True)
    v = jnp.var(x, axis=axis, keepdims=True)
    return (x - m) / jnp.sqrt(v + eps)

def _scatter_add(tgt, idx, src, axis=0):
    return tgt.at[idx].add(src)

def _segment_sum(src, seg, n):
    return jax.ops.segment_sum(src, seg, n)
kernel_name = 'mk_seq_preln_d1_jaxref_r8_e9e95e'

def setup_inputs(seed: int=0):
    np.random.seed(seed)
    _w = jnp.asarray

    def _L0_attn_setup():
        import jax, jax.numpy as jnp
        import numpy as np
        N, L, D, A, F, B = (4, 512, 128, 128, 512, 8)
        EPS_LN = 1e-06
        EPS_Z = 1e-06

        def _layernorm(x, scale, bias):
            m = jnp.mean(x, axis=-1, keepdims=True)
            v = jnp.mean(jnp.square(x - m), axis=-1, keepdims=True)
            return (x - m) * jax.lax.rsqrt(v + EPS_LN) * scale + bias

        def _block(x, p):
            Wq, bq, Wk, bk, Wv, bv, Wo, bo, ln1_s, ln1_b, Wf1, bf1, Wf2, bf2, ln2_s, ln2_b = p
            residual = x
            q = jnp.einsum('nld,da->nla', x, Wq) + bq
            k = jnp.einsum('nld,da->nla', x, Wk) + bk
            v = jnp.einsum('nld,da->nla', x, Wv) + bv
            Q = jax.nn.elu(q) + 1.0
            K = jax.nn.elu(k) + 1.0
            KV = jnp.einsum('nsh,nsh->nh', K, v)
            Ksum = jnp.sum(K, axis=1)
            Z = 1.0 / (Q * Ksum[:, None, :] + EPS_Z)
            V = Q * KV[:, None, :] * Z
            attn = jax.nn.gelu(jnp.einsum('nla,ad->nld', V, Wo) + bo)
            x = _layernorm(attn + residual, ln1_s, ln1_b)
            residual = x
            h = jax.nn.gelu(jnp.einsum('nld,df->nlf', x, Wf1) + bf1)
            ff = jax.nn.gelu(jnp.einsum('nlf,fd->nld', h, Wf2) + bf2)
            x = _layernorm(ff + residual, ln2_s, ln2_b)
            return (x, None)
        key = jax.random.key(seed)
        ks = jax.random.split(key, 10)
        s = 0.02
        x = jax.random.normal(ks[0], (N, L, D), dtype=jnp.float32)
        Wq = jax.random.normal(ks[1], (B, D, A), dtype=jnp.float32) * s
        Wk = jax.random.normal(ks[2], (B, D, A), dtype=jnp.float32) * s
        Wv = jax.random.normal(ks[3], (B, D, A), dtype=jnp.float32) * s
        Wo = jax.random.normal(ks[4], (B, A, D), dtype=jnp.float32) * s
        Wf1 = jax.random.normal(ks[5], (B, D, F), dtype=jnp.float32) * s
        Wf2 = jax.random.normal(ks[6], (B, F, D), dtype=jnp.float32) * s
        return {'x': x, 'Wq': Wq, 'bq': jnp.zeros((B, A), jnp.float32), 'Wk': Wk, 'bk': jnp.zeros((B, A), jnp.float32), 'Wv': Wv, 'bv': jnp.zeros((B, A), jnp.float32), 'Wo': Wo, 'bo': jnp.zeros((B, D), jnp.float32), 'ln1_s': jnp.ones((B, D), jnp.float32), 'ln1_b': jnp.zeros((B, D), jnp.float32), 'Wf1': Wf1, 'bf1': jnp.zeros((B, F), jnp.float32), 'Wf2': Wf2, 'bf2': jnp.zeros((B, D), jnp.float32), 'ln2_s': jnp.ones((B, D), jnp.float32), 'ln2_b': jnp.zeros((B, D), jnp.float32)}
    _L0_attn_in = _L0_attn_setup()

    def _L0_ffn_setup():
        import jax, jax.numpy as jnp
        import numpy as np
        DIM = 128
        DEPTH = 6
        HEADS = 16
        DIM_HEAD = 64
        WINDOW = 32
        INNER = HEADS * DIM_HEAD
        DIM_INNER = int(DIM * 4 * 2 / 3)
        QK_SCALE = 8.0

        def shift_tokens(t):
            a, s = jnp.split(t, 2, -1)
            s = jnp.pad(s, ((0, 0), (1, 0), (0, 0)))[:, :-1]
            return jnp.concatenate([a, s], -1)

        def l2norm(t):
            return t / jnp.maximum(jnp.linalg.norm(t, axis=-1, keepdims=True), 1e-12)

        def rotate_half(x):
            x1, x2 = jnp.split(x, 2, -1)
            return jnp.concatenate([-x2, x1], -1)

        def rotary_tables(n):
            half = jnp.arange(0, DIM_HEAD, 2, dtype=jnp.float32)
            inv_freq = 1.0 / 10000.0 ** (half / DIM_HEAD)
            t = jnp.arange(n, dtype=jnp.float32)
            freqs = t[:, None] * inv_freq[None, :]
            freqs = jnp.concatenate([freqs, freqs], -1)
            base_scale = (half + 0.4 * DIM_HEAD) / (1.4 * DIM_HEAD)
            power = (t - n // 2) / (WINDOW // 2)
            scale = base_scale[None, :] ** power[:, None]
            scale = jnp.concatenate([scale, scale], -1)
            return (freqs, scale)

        def local_attention(q, k, v):
            b, h, n, d = q.shape
            w = WINDOW
            nw = n // w
            bq = q.reshape(b, h, nw, w, d)
            bk = k.reshape(b, h, nw, w, d)
            bv = v.reshape(b, h, nw, w, d)

            def look(t):
                p = jnp.pad(t, ((0, 0), (0, 0), (1, 0), (0, 0), (0, 0)))
                return jnp.concatenate([p[:, :, :nw], p[:, :, 1:]], axis=3)
            bk2, bv2 = (look(bk), look(bv))
            seq = jnp.arange(n).reshape(nw, w)
            seq_p = jnp.pad(seq, ((1, 0), (0, 0)), constant_values=-1)
            jt = jnp.concatenate([seq_p[:nw], seq_p[1:]], axis=1)
            it = seq[:, :, None]
            jb = jt[:, None, :]
            mask = (it < jb) | (it > jb + w) | (jb == -1)
            sim = jnp.einsum('bhwie,bhwje->bhwij', bq, bk2) * QK_SCALE
            sim = jnp.where(mask, -jnp.finfo(sim.dtype).max, sim)
            attn = jax.nn.softmax(sim, -1)
            out = jnp.einsum('bhwij,bhwje->bhwie', attn, bv2)
            return out.reshape(b, h, n, d)

        def attn_layer(x, Wqkv, qs, ksc, Wo):
            b, n, _ = x.shape
            qkv = x @ Wqkv
            q, k, v = jnp.split(qkv, 3, -1)
            sh = lambda t: t.reshape(b, n, HEADS, DIM_HEAD).transpose(0, 2, 1, 3)
            q, k, v = (sh(q), sh(k), sh(v))
            q = l2norm(q) * qs
            k = l2norm(k) * ksc
            freqs, scale = rotary_tables(n)
            cos, sin = (jnp.cos(freqs), jnp.sin(freqs))
            q = q * cos * scale + rotate_half(q) * sin * scale
            inv = 1.0 / scale
            k = k * cos * inv + rotate_half(k) * sin * inv
            out = local_attention(q, k, v)
            out = out.transpose(0, 2, 1, 3).reshape(b, n, INNER)
            return out @ Wo

        def ffn_layer(x, g, bln, W1, b1, W2, b2):
            mu = x.mean(-1, keepdims=True)
            var = ((x - mu) ** 2).mean(-1, keepdims=True)
            xn = (x - mu) / jnp.sqrt(var + 1e-05) * g + bln
            hg = xn @ W1 + b1
            a, gate = jnp.split(hg, 2, -1)
            return a * jax.nn.gelu(gate, approximate=False) @ W2 + b2
        key = jax.random.key(seed)
        ks = jax.random.split(key, 8)
        B, N = (2, 256)
        init = lambda k, shape: jax.random.normal(k, shape, jnp.float32) * 0.02
        return {'x': jax.random.normal(ks[0], (B, N, DIM), jnp.float32), 'Wqkv': init(ks[1], (DEPTH, DIM, 3 * INNER)), 'q_scale': jnp.ones((DEPTH, DIM_HEAD), jnp.float32), 'k_scale': jnp.ones((DEPTH, DIM_HEAD), jnp.float32), 'Wo': init(ks[2], (DEPTH, INNER, DIM)), 'ln_g': jnp.ones((DEPTH, DIM), jnp.float32), 'ln_b': jnp.zeros((DEPTH, DIM), jnp.float32), 'W1': init(ks[3], (DEPTH, DIM, 2 * DIM_INNER)), 'b1': jnp.zeros((DEPTH, 2 * DIM_INNER), jnp.float32), 'W2': init(ks[4], (DEPTH, DIM_INNER, DIM)), 'b2': jnp.zeros((DEPTH, DIM), jnp.float32)}
    _L0_ffn_in = _L0_ffn_setup()
    _d = {'L0_attn_x': _L0_attn_in['x'], 'L0_attn_Wq': _L0_attn_in['Wq'], 'L0_attn_bq': _L0_attn_in['bq'], 'L0_attn_Wk': _L0_attn_in['Wk'], 'L0_attn_bk': _L0_attn_in['bk'], 'L0_attn_Wv': _L0_attn_in['Wv'], 'L0_attn_bv': _L0_attn_in['bv'], 'L0_attn_Wo': _L0_attn_in['Wo'], 'L0_attn_bo': _L0_attn_in['bo'], 'L0_attn_ln1_s': _L0_attn_in['ln1_s'], 'L0_attn_ln1_b': _L0_attn_in['ln1_b'], 'L0_attn_Wf1': _L0_attn_in['Wf1'], 'L0_attn_bf1': _L0_attn_in['bf1'], 'L0_attn_Wf2': _L0_attn_in['Wf2'], 'L0_attn_bf2': _L0_attn_in['bf2'], 'L0_attn_ln2_s': _L0_attn_in['ln2_s'], 'L0_attn_ln2_b': _L0_attn_in['ln2_b'], 'L0_ffn_Wqkv': _L0_ffn_in['Wqkv'], 'L0_ffn_q_scale': _L0_ffn_in['q_scale'], 'L0_ffn_k_scale': _L0_ffn_in['k_scale'], 'L0_ffn_Wo': _L0_ffn_in['Wo'], 'L0_ffn_ln_g': _L0_ffn_in['ln_g'], 'L0_ffn_ln_b': _L0_ffn_in['ln_b'], 'L0_ffn_W1': _L0_ffn_in['W1'], 'L0_ffn_b1': _L0_ffn_in['b1'], 'L0_ffn_W2': _L0_ffn_in['W2'], 'L0_ffn_b2': _L0_ffn_in['b2']}
    _x0 = _d['L0_attn_x']
    _d['L0_attn_x'] = jax.random.normal(jax.random.fold_in(jax.random.key(seed), 1), (4, 1024, 128), dtype=_x0.dtype)
    del _x0
    return _d

def reference(L0_attn_x, L0_attn_Wq, L0_attn_bq, L0_attn_Wk, L0_attn_bk, L0_attn_Wv, L0_attn_bv, L0_attn_Wo, L0_attn_bo, L0_attn_ln1_s, L0_attn_ln1_b, L0_attn_Wf1, L0_attn_bf1, L0_attn_Wf2, L0_attn_bf2, L0_attn_ln2_s, L0_attn_ln2_b, L0_ffn_Wqkv, L0_ffn_q_scale, L0_ffn_k_scale, L0_ffn_Wo, L0_ffn_ln_g, L0_ffn_ln_b, L0_ffn_W1, L0_ffn_b1, L0_ffn_W2, L0_ffn_b2):

    def _L0_attn_ref(x, Wq, bq, Wk, bk, Wv, bv, Wo, bo, ln1_s, ln1_b, Wf1, bf1, Wf2, bf2, ln2_s, ln2_b):
        import jax, jax.numpy as jnp
        import numpy as np
        N, L, D, A, F, B = (4, 512, 128, 128, 512, 8)
        EPS_LN = 1e-06
        EPS_Z = 1e-06

        def _layernorm(x, scale, bias):
            m = jnp.mean(x, axis=-1, keepdims=True)
            v = jnp.mean(jnp.square(x - m), axis=-1, keepdims=True)
            return (x - m) * jax.lax.rsqrt(v + EPS_LN) * scale + bias

        def _block(x, p):
            Wq, bq, Wk, bk, Wv, bv, Wo, bo, ln1_s, ln1_b, Wf1, bf1, Wf2, bf2, ln2_s, ln2_b = p
            residual = x
            q = jnp.einsum('nld,da->nla', x, Wq) + bq
            k = jnp.einsum('nld,da->nla', x, Wk) + bk
            v = jnp.einsum('nld,da->nla', x, Wv) + bv
            Q = jax.nn.elu(q) + 1.0
            K = jax.nn.elu(k) + 1.0
            KV = jnp.einsum('nsh,nsh->nh', K, v)
            Ksum = jnp.sum(K, axis=1)
            Z = 1.0 / (Q * Ksum[:, None, :] + EPS_Z)
            V = Q * KV[:, None, :] * Z
            attn = jax.nn.gelu(jnp.einsum('nla,ad->nld', V, Wo) + bo)
            x = _layernorm(attn + residual, ln1_s, ln1_b)
            residual = x
            h = jax.nn.gelu(jnp.einsum('nld,df->nlf', x, Wf1) + bf1)
            ff = jax.nn.gelu(jnp.einsum('nlf,fd->nld', h, Wf2) + bf2)
            x = _layernorm(ff + residual, ln2_s, ln2_b)
            return (x, None)
        params = (Wq, bq, Wk, bk, Wv, bv, Wo, bo, ln1_s, ln1_b, Wf1, bf1, Wf2, bf2, ln2_s, ln2_b)
        out, _ = jax.lax.scan(_block, x, params)
        return out

    def _L0_ffn_ref(x, Wqkv, q_scale, k_scale, Wo, ln_g, ln_b, W1, b1, W2, b2):
        import jax, jax.numpy as jnp
        import numpy as np
        DIM = 128
        DEPTH = 6
        HEADS = 16
        DIM_HEAD = 64
        WINDOW = 32
        INNER = HEADS * DIM_HEAD
        DIM_INNER = int(DIM * 4 * 2 / 3)
        QK_SCALE = 8.0

        def shift_tokens(t):
            a, s = jnp.split(t, 2, -1)
            s = jnp.pad(s, ((0, 0), (1, 0), (0, 0)))[:, :-1]
            return jnp.concatenate([a, s], -1)

        def l2norm(t):
            return t / jnp.maximum(jnp.linalg.norm(t, axis=-1, keepdims=True), 1e-12)

        def rotate_half(x):
            x1, x2 = jnp.split(x, 2, -1)
            return jnp.concatenate([-x2, x1], -1)

        def rotary_tables(n):
            half = jnp.arange(0, DIM_HEAD, 2, dtype=jnp.float32)
            inv_freq = 1.0 / 10000.0 ** (half / DIM_HEAD)
            t = jnp.arange(n, dtype=jnp.float32)
            freqs = t[:, None] * inv_freq[None, :]
            freqs = jnp.concatenate([freqs, freqs], -1)
            base_scale = (half + 0.4 * DIM_HEAD) / (1.4 * DIM_HEAD)
            power = (t - n // 2) / (WINDOW // 2)
            scale = base_scale[None, :] ** power[:, None]
            scale = jnp.concatenate([scale, scale], -1)
            return (freqs, scale)

        def local_attention(q, k, v):
            b, h, n, d = q.shape
            w = WINDOW
            nw = n // w
            bq = q.reshape(b, h, nw, w, d)
            bk = k.reshape(b, h, nw, w, d)
            bv = v.reshape(b, h, nw, w, d)

            def look(t):
                p = jnp.pad(t, ((0, 0), (0, 0), (1, 0), (0, 0), (0, 0)))
                return jnp.concatenate([p[:, :, :nw], p[:, :, 1:]], axis=3)
            bk2, bv2 = (look(bk), look(bv))
            seq = jnp.arange(n).reshape(nw, w)
            seq_p = jnp.pad(seq, ((1, 0), (0, 0)), constant_values=-1)
            jt = jnp.concatenate([seq_p[:nw], seq_p[1:]], axis=1)
            it = seq[:, :, None]
            jb = jt[:, None, :]
            mask = (it < jb) | (it > jb + w) | (jb == -1)
            sim = jnp.einsum('bhwie,bhwje->bhwij', bq, bk2) * QK_SCALE
            sim = jnp.where(mask, -jnp.finfo(sim.dtype).max, sim)
            attn = jax.nn.softmax(sim, -1)
            out = jnp.einsum('bhwij,bhwje->bhwie', attn, bv2)
            return out.reshape(b, h, n, d)

        def attn_layer(x, Wqkv, qs, ksc, Wo):
            b, n, _ = x.shape
            qkv = x @ Wqkv
            q, k, v = jnp.split(qkv, 3, -1)
            sh = lambda t: t.reshape(b, n, HEADS, DIM_HEAD).transpose(0, 2, 1, 3)
            q, k, v = (sh(q), sh(k), sh(v))
            q = l2norm(q) * qs
            k = l2norm(k) * ksc
            freqs, scale = rotary_tables(n)
            cos, sin = (jnp.cos(freqs), jnp.sin(freqs))
            q = q * cos * scale + rotate_half(q) * sin * scale
            inv = 1.0 / scale
            k = k * cos * inv + rotate_half(k) * sin * inv
            out = local_attention(q, k, v)
            out = out.transpose(0, 2, 1, 3).reshape(b, n, INNER)
            return out @ Wo

        def ffn_layer(x, g, bln, W1, b1, W2, b2):
            mu = x.mean(-1, keepdims=True)
            var = ((x - mu) ** 2).mean(-1, keepdims=True)
            xn = (x - mu) / jnp.sqrt(var + 1e-05) * g + bln
            hg = xn @ W1 + b1
            a, gate = jnp.split(hg, 2, -1)
            return a * jax.nn.gelu(gate, approximate=False) @ W2 + b2
        for i in range(DEPTH):
            x = attn_layer(shift_tokens(x), Wqkv[i], q_scale[i], k_scale[i], Wo[i]) + x
            x = ffn_layer(shift_tokens(x), ln_g[i], ln_b[i], W1[i], b1[i], W2[i], b2[i]) + x
        return x
    x = L0_attn_x
    x = x + _L0_attn_ref(_layernorm(x, axis=-1), L0_attn_Wq, L0_attn_bq, L0_attn_Wk, L0_attn_bk, L0_attn_Wv, L0_attn_bv, L0_attn_Wo, L0_attn_bo, L0_attn_ln1_s, L0_attn_ln1_b, L0_attn_Wf1, L0_attn_bf1, L0_attn_Wf2, L0_attn_bf2, L0_attn_ln2_s, L0_attn_ln2_b)
    x = x + _L0_ffn_ref(_layernorm(x, axis=-1), L0_ffn_Wqkv, L0_ffn_q_scale, L0_ffn_k_scale, L0_ffn_Wo, L0_ffn_ln_g, L0_ffn_ln_b, L0_ffn_W1, L0_ffn_b1, L0_ffn_W2, L0_ffn_b2)
    return x

_drawn_inputs = setup_inputs


def setup_inputs(seed=0):
    import zlib

    import numpy as np

    out = dict(_drawn_inputs(seed))
    spreads = {'L0_attn_bq': (0.0, 2.0),
     'L0_attn_bk': (0.0, 2.0),
     'L0_attn_bv': (0.0, 0.477),
     'L0_attn_bo': (0.0, 0.1),
     'L0_attn_ln1_s': (1.0, 0.2),
     'L0_attn_ln1_b': (0.0, 0.1),
     'L0_attn_bf1': (0.0, 0.498),
     'L0_attn_bf2': (0.0, 0.1),
     'L0_attn_ln2_s': (1.0, 0.2),
     'L0_attn_ln2_b': (0.0, 0.1),
     'L0_ffn_q_scale': (1.0, 0.6),
     'L0_ffn_k_scale': (1.0, 0.6),
     'L0_ffn_ln_g': (1.0, 0.6),
     'L0_ffn_ln_b': (0.0, 0.8),
     'L0_ffn_b1': (0.0, 0.8),
     'L0_ffn_b2': (0.0, 0.1)}
    factors = {'L0_attn_Wq': 64.0,
     'L0_attn_Wk': 8.0,
     'L0_attn_Wv': 4.42,
     'L0_attn_Wo': 3.087,
     'L0_ffn_W1': 5.405,
     'L0_ffn_W2': 5.36}
    for name, (base, spread) in spreads.items():
        noise = np.random.default_rng([zlib.crc32(name.encode()), seed]).standard_normal(out[name].shape)
        drawn = base * np.exp(spread * noise) if base else spread * noise
        out[name] = jnp.asarray(drawn.astype(out[name].dtype))
    for name, factor in factors.items():
        out[name] = (out[name] * factor).astype(out[name].dtype)
    return out
```

```python
from contextlib import ExitStack

import numpy as np
import concourse.bass as bass
from concourse import mybir

F32 = mybir.dt.float32
ALU = mybir.AluOpType
ACT = mybir.ActivationFunctionType
AX_X = mybir.AxisListType.X
ds = bass.ds

P = 128
NB, SEQ, D = 4, 1024, 128
BLOCKS, FA = 8, 512
MA = FA // P
LAYERS, HEADS, DH, WIN = 6, 16, 64, 32
INNER = HEADS * DH
HID = int(D * 4 * 2 / 3)
MF = -(-HID // P)
FW = [min(P, HID - P * m) for m in range(MF)]
COL = 512
UT = SEQ // COL
TS = SEQ // P
NT = NB * TS
SP1 = SEQ + 1
NP = HEADS // 2
QKC = 2 * INNER // COL
NEG = -1.0e30
EPS_PRE, EPS_A, EPS_F, EPS_Z = 1e-5, 1e-6, 1e-5, 1e-6
NORM_MIN = 1e-24
QK_SCALE = 8.0

A1_B = 3 * D
A1_W = A1_B + 3
A2_F1, A2_F2 = D, D + FA
A2_V = A2_F2 + MA * D
A2_BO, A2_S1, A2_B1, A2_BF1 = A2_V, A2_V + 1, A2_V + 2, A2_V + 3
A2_BF2 = A2_BF1 + MA
A2_S2, A2_B2 = A2_BF2 + 1, A2_BF2 + 2
A2_W = A2_B2 + 1
B_WO = 3 * INNER
B_SC = B_WO + NP * D
B_W = B_SC + 4 * DH
F_W2 = 2 * HID
F_G = F_W2 + MF * D
F_B = F_G + 1
F_BA = F_B + 1
F_BG = F_BA + MF
F_B2 = F_BG + MF
F_W = F_B2 + 1


def build(nc, xT, wa1, wa2, wb, wf, rot, mask, outT):
    with ExitStack() as ctx:
        def sb(name, shape):
            return ctx.enter_context(nc.sbuf_tensor(name, shape, F32))

        def sem(name):
            return ctx.enter_context(nc.semaphore(name))

        def pair(name):
            return [sem(f"{name}_{u}") for u in range(UT)]

        ps = ctx.enter_context(nc.psum_tensor("ps", [P, 8, COL], F32))

        X = sb("X", [P, NB * SP1])
        Y = sb("Y", [P, NB * SP1])
        keep = sb("keep", [P, NB * SEQ])
        ident = sb("ident", [P, P])
        power = sb("power", [P, 2 * HEADS])
        WB = sb("WB", [P, B_W])
        WF = sb("WF", [P, F_W])
        rotary = sb("rotary", [P, 4, TS, DH])
        tables = sb("tables", [P, 4, TS, DH])
        maskt = sb("maskt", [P, TS, 2 * WIN])
        inside = sb("inside", [P, TS])
        stats = sb("stats", [P, UT, 4, 6])
        mv = sb("mv", [P, UT, 4, 2])
        ve = sb("ve", [P, UT, 4])
        rstd = sb("rstd", [P, UT, 4])
        kvp = sb("kvp", [P, UT, 2])
        kvs = sb("kvs", [P, NB, 2])
        bias1 = sb("bias1", [P, 3])
        ssq = sb("ssq", [P, 2 * HEADS])
        ssc = sb("ssc", [P, 2 * HEADS])
        rinv = sb("rinv", [P, 2 * HEADS])
        mx = sb("mx", [P, HEADS])
        rs = sb("rs", [P, HEADS])
        rr = sb("rr", [P, HEADS])

        arena = sb("arena", [P, 24600])

        def carve(sizes):
            at, got = 0, []
            for n in sizes:
                got.append(arena[:, at:at + n])
                at += n
            return got

        (Wa1, Wa2, Qf, *rest) = carve([A1_W, A2_W, NB * SEQ] + [COL] * (UT * 13))
        ta = {k: [rest[i * UT + u] for u in range(UT)]
              for i, k in enumerate(["mk", "ek", "K", "den", "Vb", "g", "z", "zn", "x1"])}
        ha = [arena[:, A1_W + A2_W + NB * SEQ + COL * (18 + MA * u):][:, 0:MA * COL]
              .rearrange("p (m n) -> p m n", m=MA) for u in range(UT)]
        (t1a, t1b, t2, sq, sc, pe_, pt, PTd, qTf, kTf, va, vb, vsa, vsb, OTf, xsa, xsb) = carve(
            [2 * INNER] * 4 + [INNER] * 3 + [2 * HEADS * P] + [INNER] + [NP * (WIN + P)] + [INNER] * 4
            + [INNER] + [P] * 2)
        t1 = [t1a, t1b]
        v_, vs_ = [va, vb], [vsa, vsb]
        xs_ = [xsa, xsb]
        qT = qTf.rearrange("p (c t) -> p c t", c=NP)
        kT = kTf.rearrange("p (c t) -> p c t", c=NP)
        OT = OTf.rearrange("p (c t) -> p c t", c=NP)
        fa = arena[:, 0:8 * INNER].rearrange("p (k n) -> p k n", n=COL)
        tf = {k: [fa[:, i * UT + u, :] for u in range(UT)] for i, k in enumerate(["xs", "zn", "xn"])}
        gf = [fa[:, 6 + u, :] for u in range(UT)]
        hf = [fa[:, 8 + MF * u:8 + MF * u + MF, :] for u in range(UT)]

        loaded, consts = sem("loaded"), sem("consts")
        la1, la2, lb, lf = sem("wa1_in"), sem("wa2_in"), sem("wb_in"), sem("wf_in")
        stored = sem("stored")
        x_done = pair("x_done")

        LN = {k: {s: pair(f"{k}_{s}") for s in ("z", "tr", "stat", "rstd", "zn", "tb")}
              for k in ("pre", "n1", "n2", "nf")}
        xlo, xhi = pair("xs_lo"), LN["nf"]["z"]
        kept = pair("kept")
        kvq, mins, exps, kq_used = pair("kvq_mm"), pair("mins"), pair("exps"), pair("kvq_used")
        rounded = pair("q_rounded")
        ksum = sem("seq_sums")
        biased = sem("bias1_ready")
        vprep, vready, wo_mm, ga = pair("v_chain"), pair("v_ready"), pair("wo_mm"), pair("attn_gelu")
        x1_r, f1_mm, h_r, f2_mm, g2 = pair("x1_r"), pair("f1_mm"), pair("h_r"), pair("f2_mm"), pair("ff_gelu")

        xn_r, ag_mm, gate_r, hf_r, o_mm = map(pair, ("xn_r", "ag_mm", "gate_r", "hf_r", "o_mm"))
        finals, passed = sem("finals"), sem("waits_passed")

        (tab_r, xs_r, qk_mm, v_mm, sq_r, rot_r, add_r, red_r, ssc_r, rinv_r, qk_r, tr_mm, shift_r, tr_ev,
         s_mm, s_rd, max_r, sub_r, exp_r, sum_r, rec_r, p_r, pt_r, ptd_r, pv_mm, ot_r, wo_r, y_r, v_r,
         vs_in) = map(sem, (
             "tables_ready", "xs_ready", "qk_mm", "v_mm", "squares", "rotated", "added", "sumsq",
             "sumsq_scaled", "rinv_ready", "qk_ready", "transposed", "keys_shifted", "transposes_out",
             "scores_mm", "scores_masked", "max_ready", "shifted", "exp_ready", "sum_ready", "recip_ready",
             "probs_ready", "probsT_ready", "probsT_wide", "pv_mm", "ot_ready", "wo_done", "y_ready",
             "v_ready_b", "vshift_in"))

        def seq_col(b, t):
            return b * SP1 + 1 + t

        def tile_col(n):
            return n * P + n // TS + 1

        def hold(eng, s, v):
            eng.wait_ge(s, v)
            eng.sem_inc(passed, 1)

        def c4(ap):
            return ap.rearrange("p (j t) -> p j t", j=4)

        def ln_turn(pe, k, u, v, src, bank):
            pe.wait_ge(LN[k]["z"][u], v)
            for j in range(4):
                i = pe.transpose(ps[:, bank, j * P:(j + 1) * P], src[:, j * P:(j + 1) * P], ident[:, :])
            i.then_inc(LN[k]["tr"][u], 1)

        def ln_stats(dve, k, u, v, bank, eps):
            st = LN[k]["stat"][u]
            dve.wait_ge(LN[k]["tr"][u], v + 1)
            for j in range(4):
                i = dve.bn_stats(stats[:, u, j, :], ps[:, bank, j * P:(j + 1) * P])
            i.then_inc(st, 1)

        def ln_aggr(dve, k, u, v, eps):
            st = LN[k]["stat"][u]
            hold(dve, st, 3 * v - 2)
            for j in range(4):
                i = dve.bn_aggr(mv[:, u, j, :], stats[:, u, j, :])
            i.then_inc(st, 1)
            dve.wait_ge(st, 3 * v - 1)
            dve.tensor_scalar(ve[:, u, :], mv[:, u, :, 1], eps, None, ALU.add).then_inc(st, 1)

        def ln_rstd(pool, k, u, v):
            pool.wait_ge(LN[k]["stat"][u], 3 * v)
            pool.tensor_tensor(rstd[:, u, :], ve[:, u, :], power[:, 0:4], ALU.pow)\
                .then_inc(LN[k]["rstd"][u], 1)

        def ln_norm(dve, k, u, v, bank, dst):
            dve.wait_ge(LN[k]["rstd"][u], v)
            for j in range(4):
                i = dve.tensor_scalar(dst[:, j * P:(j + 1) * P], ps[:, bank, j * P:(j + 1) * P],
                                      mv[:, u, j, 0:1], rstd[:, u, j:j + 1], ALU.subtract, ALU.mult)
            i.then_inc(LN[k]["zn"][u], 1)

        def ln_back(pe, k, u, v, src, bank):
            pe.wait_ge(LN[k]["zn"][u], v)
            for j in range(4):
                i = pe.transpose(ps[:, bank, j * P:(j + 1) * P], src[:, j * P:(j + 1) * P], ident[:, :])
            i.then_inc(LN[k]["tb"][u], 1)

        U = range(UT)
        bank = [[4 * u + i for i in range(4)] for u in U]
        block = ctx.enter_context(nc.Block())

        @block.sync
        def _(sp):
            for s in (v_mm, wo_r, v_r, s_rd, y_r, ptd_r, red_r, s_mm, pt_r, pv_mm, vs_in, add_r,
                      *kq_used, *hf_r, *kept, *x_done, *(q for k in LN.values() for q in k["tr"])):
                sp.sem_inc(s, 1)
            sp.dma_start(keep[:, :], xT).then_inc(loaded, 16)
            sp.dma_start(rotary[:, :, :, :].rearrange("p a b c -> p (a b c)"), rot).then_inc(loaded, 16)
            sp.dma_start(maskt[:, :, :].rearrange("p a b -> p (a b)"), mask[:, 0:TS * 2 * WIN]).then_inc(loaded, 16)
            sp.dma_start(inside[:, :], mask[:, TS * 2 * WIN:]).then_inc(loaded, 16)
            with sp.Fori(0, BLOCKS) as l:
                for u in U:
                    hold(sp, kq_used[u], NB * l + 1)
                sp.dma_start(Wa1, wa1[ds(l * P, P), :]).then_inc(la1, 16)
                for u in U:
                    hold(sp, x_done[u], NB * (l + 1) + 1)
                sp.dma_start(Wa2, wa2[ds(l * P, P), :]).then_inc(la2, 16)
            with sp.Fori(0, LAYERS) as l:
                hold(sp, v_mm, NT * 2 * l + 1)
                hold(sp, wo_r, NT * l + 1)
                sp.dma_start(WB[:, :], wb[ds(l * P, P), :]).then_inc(lb, 16)
                for u in U:
                    hold(sp, x_done[u], NB * (BLOCKS + 2 + l) + 1)
                sp.dma_start(WF[:, :], wf[ds(l * P, P), :]).then_inc(lf, 16)

                def vshift(n, par):
                    g = l * NT + n
                    hold(sp, v_r, 2 * g + 3)
                    sp.dma_start(vs_[par][WIN:P, :], v_[par][0:P - WIN, :]).then_inc(vs_in, 16)
                    sp.dma_start(vs_[par][0:WIN, :], v_[1 - par][P - WIN:P, :]).then_inc(vs_in, 16)

                with sp.Fori(0, NT // 2) as j:
                    vshift(2 * j, 0)
                    vshift(2 * j + 1, 1)
            sp.wait_ge(finals, NB)
            sp.dma_start(outT, keep[:, :]).then_inc(stored, 16)
            sp.wait_ge(stored, 16)

        @block.gpsimd
        def _(pool):
            pool.memset(ident[:, :], 0.0).then_inc(consts, 1)
            pool.memset(power[:, :], -0.5).then_inc(consts, 1)
            pool.wait_ge(consts, 1)
            pool.affine_select(out=ident[:, :], in_=ident[:, :], compare_op=ALU.not_equal, fill=1.0, base=0,
                               pattern=[[-1, P]], channel_multiplier=1).then_inc(consts, 1)
            pool.memset(X[:, :], 0.0).then_inc(consts, 1)
            pool.memset(Y[:, :], 0.0).then_inc(consts, 1)
            pool.wait_ge(consts, 5)

            def pre_norm(k):
                with pool.Fori(0, NB) as b:
                    for u in U:
                        ln_rstd(pool, "pre", u, k * NB + b + 1)

            pre_norm(0)
            with pool.Fori(0, BLOCKS) as l:
                with pool.Fori(0, NB) as b:
                    for k in ("n1", "n2"):
                        for u in U:
                            ln_rstd(pool, k, u, l * NB + b + 1)
            pre_norm(1)
            for u in U:
                pool.wait_ge(x_done[u], NB * (BLOCKS + 2) + 1)
            pool.memset(PTd, 0.0).then_inc(consts, 1)
            pool.memset(kTf, 0.0).then_inc(consts, 1)
            pool.memset(v_[1], 0.0).then_inc(consts, 1)
            with pool.Fori(0, LAYERS) as l:
                def probs_sub(n):
                    g = l * NT + n
                    pool.wait_ge(max_r, g + 1)
                    s3 = sc.rearrange("p (h k) -> p h k", h=HEADS)
                    pool.tensor_tensor(s3, s3, mx[:, :].unsqueeze(2).to_broadcast([P, HEADS, 2 * WIN]),
                                       ALU.subtract).then_inc(sub_r, 1)

                def probs_norm(n):
                    g = l * NT + n
                    pool.wait_ge(rec_r, g + 1)
                    p3 = pe_.rearrange("p (h k) -> p h k", h=HEADS)
                    pool.tensor_tensor(p3, p3, rr[:, :].unsqueeze(2).to_broadcast([P, HEADS, 2 * WIN]),
                                       ALU.mult).then_inc(p_r, 1)

                def add(n, par, c):
                    g = l * NT + n
                    pool.wait_ge(rot_r, QKC * g + c + 1)
                    w = slice(c * COL, (c + 1) * COL)
                    pool.tensor_tensor(t1[par][:, w], t1[par][:, w], t2[:, w], ALU.add).then_inc(add_r, 1)

                def norms(n):
                    g = l * NT + n
                    pool.wait_ge(ssc_r, 2 * g + 2)
                    pool.tensor_tensor(rinv[:, :], ssc[:, :], power[:, :], ALU.pow).then_inc(rinv_r, 1)

                def step(n, par, before, after):
                    if before:
                        probs_sub(n - 1)
                    if after:
                        add(n + 1, 1 - par, 0)
                        add(n + 1, 1 - par, 1)
                    if before:
                        probs_norm(n - 1)
                    if after:
                        add(n + 1, 1 - par, 2)
                        add(n + 1, 1 - par, 3)
                        norms(n + 1)

                step(-1, 1, False, True)
                step(0, 0, False, True)
                with pool.Fori(0, NT // 2 - 1) as j:
                    step(2 * j + 1, 1, True, True)
                    step(2 * j + 2, 0, True, True)
                step(NT - 1, 1, True, False)
                step(NT, 0, True, False)
                with pool.Fori(0, NB) as b:
                    for u in U:
                        ln_rstd(pool, "nf", u, l * NB + b + 1)

        @block.tensor
        def _(pe):
            pe.wait_ge(consts, 3)

            def pre_norm(k):
                with pe.Fori(0, NB) as b:
                    v = k * NB + b + 1
                    for u in U:
                        ln_turn(pe, "pre", u, v, ta["z"][u], bank[u][0])
                    for u in U:
                        pe.wait_ge(x_done[u], k * NB * (BLOCKS + 1) + b + 1)
                        ln_back(pe, "pre", u, v, ta["zn"][u], bank[u][1])

            pre_norm(0)
            with pe.Fori(0, BLOCKS) as l:
                pe.wait_ge(la1, 16 * (l + 1))
                for u in U:
                    hold(pe, x_done[u], NB * (l + 1) + 1)
                with pe.Fori(0, NB) as b:
                    it = l * NB + b
                    for u in U:
                        pe.wait_ge(kq_used[u], it + 1)
                        xcol = X[:, ds(seq_col(b, COL * u), COL)]
                        for i, w in enumerate((1, 0, 2)):
                            m = pe.matmul(ps[:, bank[u][i], :], Wa1[:, w * D:(w + 1) * D], xcol,
                                          start=True, stop=True)
                        m.then_inc(kvq[u], 1)
                hold(pe, la2, 16 * (l + 1))
                with pe.Fori(0, NB) as b:
                    v = l * NB + b + 1
                    for u in U:
                        pe.wait_ge(vready[u], v)
                        pe.matmul(ps[:, bank[u][0], :], Wa2[:, 0:D], ta["Vb"][u], start=True, stop=True)\
                            .then_inc(wo_mm[u], 1)
                    for u in U:
                        ln_turn(pe, "n1", u, v, ta["z"][u], bank[u][1])
                    for u in U:
                        ln_back(pe, "n1", u, v, ta["zn"][u], bank[u][2])
                    for u in U:
                        pe.wait_ge(x1_r[u], v)
                        for m in range(MA):
                            pe.matmul(ps[:, bank[u][(3 + m) % 4], :], Wa2[:, A2_F1 + m * P:A2_F1 + (m + 1) * P],
                                      ta["x1"][u], start=True, stop=True).then_inc(f1_mm[u], 1)
                    for u in U:
                        for m in range(MA):
                            pe.wait_ge(h_r[u], MA * (v - 1) + m + 1)
                            i = pe.matmul(ps[:, bank[u][3], :], Wa2[:, A2_F2 + m * D:A2_F2 + (m + 1) * D],
                                          ha[u][:, m, :], start=(m == 0), stop=(m == MA - 1))
                        i.then_inc(f2_mm[u], 1)
                    for u in U:
                        ln_turn(pe, "n2", u, v, ta["z"][u], bank[u][0])
                    for u in U:
                        ln_back(pe, "n2", u, v, ta["zn"][u], bank[u][1])
            pre_norm(1)

            pe.wait_ge(consts, 8)
            with pe.Fori(0, LAYERS) as l:
                def project(n, par, c):
                    return pe.matmul(ps[:, c % 2, :], xs_[par], WB[:, c * COL:(c + 1) * COL],
                                     start=True, stop=True)

                def project_qk(n, par):
                    g = l * NT + n
                    pe.wait_ge(xs_r, 2 * g + 2)
                    for c in range(QKC):
                        if c < 2:
                            pe.wait_ge(v_r, 2 * g + 1)
                        else:
                            pe.wait_ge(rot_r, QKC * g + c - 1)
                            pe.wait_ge(sq_r, QKC * g + c - 1)
                        project(n, par, c).then_inc(qk_mm, 1)

                def project_v(n, par):
                    g = l * NT + n
                    for c in range(2):
                        pe.wait_ge(rot_r, QKC * g + c + 3)
                        pe.wait_ge(sq_r, QKC * g + c + 3)
                        project(n, par, QKC + c).then_inc(v_mm, 1)

                def turn(n, par):
                    g = l * NT + n
                    pe.wait_ge(qk_r, g + 1)
                    for r in range(4):
                        if r >= 2:
                            pe.wait_ge(tr_ev, 4 * g + r - 1)
                        for j in range(4):
                            c = 4 * r + j
                            i = pe.transpose(ps[:, 2 + r % 2, j * P:(j + 1) * P],
                                             t1[par][:, c * P:(c + 1) * P], ident[:, :])
                        i.then_inc(tr_mm, 1)

                def scores(n):
                    g = l * NT + n
                    pe.wait_ge(s_rd, g + 1)
                    hold(pe, tr_ev, 4 * g + 4)
                    for w in range(4):
                        for h in range(HEADS):
                            r = 64 * (h % 2)
                            i = pe.matmul(ps[WIN * w:WIN * (w + 1), 4 + h % 2, (h // 2) * 64:(h // 2) * 64 + 64],
                                          qT[r:r + 64, h // 2, WIN * w:WIN * (w + 1)],
                                          kT[r:r + 64, h // 2, WIN * w:WIN * (w + 2)], start=True, stop=True)
                    i.then_inc(s_mm, 1)

                def attend(n, par):
                    g = l * NT + n
                    pe.wait_ge(ptd_r, g + 2)
                    pe.wait_ge(vs_in, 32 * (g + 1) + 1)
                    pe.wait_ge(y_r, g + 1)
                    pw = PTd.rearrange("p (a c k q) -> p a c k q", a=2, c=NP, k=2)
                    for c in range(NP):
                        for part, val in ((1, v_[par]), (0, vs_[par])):
                            for a in range(2):
                                h = 2 * c + a
                                i = pe.matmul(ps[64 * a:64 * a + 64, 6 + c // 4, (c % 4) * P:(c % 4 + 1) * P],
                                              val[:, h * DH:(h + 1) * DH], pw[:, a, c, part, :],
                                              start=(part == 1), stop=(part == 0))
                        if c % 4 == 3:
                            i.then_inc(pv_mm, 1)
                    for c in range(NP):
                        if c % 4 == 0:
                            pe.wait_ge(ot_r, 2 * g + 1 + c // 4)
                        i = pe.matmul(ps[:, 6, 0:P], WB[:, B_WO + c * D:B_WO + (c + 1) * D], OT[:, c, :],
                                      start=(c == 0), stop=(c == NP - 1))
                    i.then_inc(wo_r, 1)

                def step(n, par, before, here, after):
                    if after:
                        project_qk(n + 1, 1 - par)
                    if here:
                        turn(n, par)
                        scores(n)
                    if before:
                        attend(n - 1, 1 - par)
                    if after:
                        project_v(n + 1, 1 - par)

                pe.wait_ge(lb, 16 * (l + 1))
                step(-1, 1, False, False, True)
                step(0, 0, False, True, True)
                with pe.Fori(0, NT // 2 - 1) as j:
                    step(2 * j + 1, 1, True, True, True)
                    step(2 * j + 2, 0, True, True, True)
                step(NT - 1, 1, True, True, False)
                step(NT, 0, True, False, False)

                hold(pe, lf, 16 * (l + 1))
                with pe.Fori(0, NB) as b:
                    v = l * NB + b + 1
                    for u in U:
                        pe.wait_ge(xlo[u], v)
                        ln_turn(pe, "nf", u, v, tf["xs"][u], bank[u][0])
                    for u in U:
                        ln_back(pe, "nf", u, v, tf["zn"][u], bank[u][1])
                    for m in range(MF):
                        for u in U:
                            if m == 0:
                                pe.wait_ge(xn_r[u], v)
                            if m == 2:
                                pe.wait_ge(hf_r[u], MF * (v - 1) + 2)
                            for k in (1, 0):
                                pe.matmul(ps[0:FW[m], bank[u][(2 + 2 * m + 1 - k) % 4], :],
                                          WF[:, k * HID + m * P:k * HID + m * P + FW[m]], tf["xn"][u],
                                          start=True, stop=True).then_inc(ag_mm[u], 1)
                    for u in U:
                        for m in range(MF):
                            if m == 0:
                                pe.wait_ge(hf_r[u], MF * (v - 1) + 2 + 1)
                            elif m == 2:
                                pe.wait_ge(hf_r[u], MF * v + 1)
                            i = pe.matmul(ps[:, bank[u][0], :], WF[0:FW[m], F_W2 + m * D:F_W2 + (m + 1) * D],
                                          hf[u][0:FW[m], m, :], start=(m == 0), stop=(m == MF - 1))
                        i.then_inc(o_mm[u], 1)

        @block.scalar
        def _(act):
            def pre_norm(k):
                with act.Fori(0, NB) as b:
                    v = k * NB + b + 1
                    for u in U:
                        if k:
                            act.wait_ge(LN["pre"]["z"][u], v)
                            act.activation(keep[:, ds(b * SEQ + COL * u, COL)], ta["z"][u], ACT.Copy)\
                                .then_inc(kept[u], 1)
                    for u in U:
                        act.wait_ge(LN["pre"]["tb"][u], v)
                        act.activation(X[:, ds(seq_col(b, COL * u), COL)], ps[:, bank[u][1], :], ACT.Copy)\
                            .then_inc(x_done[u], 1)

            act.wait_ge(consts, 5)
            pre_norm(0)
            with act.Fori(0, BLOCKS) as l:
                with act.Fori(0, NB) as b:
                    v = l * NB + b + 1
                    for u in U:
                        for i, k in enumerate(("ek", "K")):
                            act.wait_ge(mins[u], 2 * v - 1 + i)
                            src = ta["mk"][u] if i == 0 else ta["den"][u]
                            act.activation(ta["ek"][u] if i == 0 else ta["Vb"][u], src, ACT.Exp)\
                                .then_inc(exps[u], 1)
                hold(act, la2, 16 * (l + 1))
                with act.Fori(0, NB) as b:
                    v = l * NB + b + 1
                    for u in U:
                        act.wait_ge(wo_mm[u], v)
                        act.activation(ta["g"][u], ps[:, bank[u][0], :], ACT.Gelu_apprx_tanh,
                                       bias=Wa2[:, A2_BO:A2_BO + 1]).then_inc(ga[u], 1)
                    for u in U:
                        act.wait_ge(LN["n1"]["tb"][u], v)
                        act.activation(ta["x1"][u], ps[:, bank[u][2], :], ACT.Identity,
                                       bias=Wa2[:, A2_B1:A2_B1 + 1], scale=Wa2[:, A2_S1:A2_S1 + 1])\
                            .then_inc(x1_r[u], 1)
                    for u in U:
                        for m in range(MA):
                            act.wait_ge(f1_mm[u], MA * (v - 1) + m + 1)
                            act.activation(ha[u][:, m, :], ps[:, bank[u][(3 + m) % 4], :], ACT.Gelu_apprx_tanh,
                                           bias=Wa2[:, A2_BF1 + m:A2_BF1 + m + 1]).then_inc(h_r[u], 1)
                    for u in U:
                        act.wait_ge(f2_mm[u], v)
                        act.activation(ta["g"][u], ps[:, bank[u][3], :], ACT.Gelu_apprx_tanh,
                                       bias=Wa2[:, A2_BF2:A2_BF2 + 1]).then_inc(g2[u], 1)
                    for u in U:
                        act.wait_ge(LN["n2"]["tb"][u], v)
                        act.activation(X[:, ds(seq_col(b, COL * u), COL)], ps[:, bank[u][1], :], ACT.Identity,
                                       bias=Wa2[:, A2_B2:A2_B2 + 1], scale=Wa2[:, A2_S2:A2_S2 + 1])\
                            .then_inc(x_done[u], 1)
            pre_norm(1)

            act.wait_ge(consts, 8)
            act.wait_ge(loaded, 64)
            with act.Fori(0, LAYERS) as l:
                def square(n, c):
                    g = l * NT + n
                    act.wait_ge(qk_mm, QKC * g + c + 1)
                    if c == 0:
                        act.wait_ge(red_r, QKC * g + 1)
                    act.activation(sq[:, c * COL:(c + 1) * COL], ps[:, c % 2, :], ACT.Square)\
                        .then_inc(sq_r, 1)

                def keys_on(n):
                    g = l * NT + n
                    act.wait_ge(s_mm, g + 1)
                    act.activation(kT[:, :, 0:WIN], kT[:, :, P:P + WIN], ACT.Copy,
                                   scale=inside[:, ds(n % TS, 1)]).then_inc(shift_r, 1)
                    act.wait_ge(shift_r, g + 1)

                def turned(n, r):
                    g = l * NT + n
                    act.wait_ge(tr_mm, 4 * g + r + 1)
                    dst = (qT[:, 4 * r:4 * r + 4, :] if r < 2 else
                           kT[:, 4 * (r - 2):4 * (r - 2) + 4, WIN:WIN + P])
                    act.activation(dst, c4(ps[:, 2 + r % 2, :]), ACT.Copy).then_inc(tr_ev, 1)

                def exponent(n):
                    g = l * NT + n
                    act.wait_ge(sub_r, g + 1)
                    act.wait_ge(pt_r, g + 1)
                    act.activation(pe_, sc, ACT.Exp).then_inc(exp_r, 1)

                def widen(n):
                    g = l * NT + n
                    act.wait_ge(pt_r, g + 2)
                    act.wait_ge(pv_mm, 2 * g + 1)
                    for w in range(4):
                        q = slice(WIN * w, WIN * (w + 1))
                        i = act.activation(PTd.rearrange("p (k q) -> p k q", q=P)[q, :, q],
                                           pt.rearrange("p (k q) -> p k q", q=WIN)[q, :, :], ACT.Copy)
                    i.then_inc(ptd_r, 1)

                def outputs(n, r):
                    g = l * NT + n
                    act.wait_ge(pv_mm, 2 * g + 1 + r + 1)
                    if r == 0:
                        act.wait_ge(wo_r, g + 1)
                    act.activation(OT[:, 4 * r:4 * r + 4, :], c4(ps[:, 6 + r, :]), ACT.Copy).then_inc(ot_r, 1)

                def values(n, par, c):
                    g = l * NT + n
                    act.wait_ge(v_mm, 2 * g + c + 2)
                    if c == 0:
                        act.wait_ge(vs_in, 32 * g + 1)
                    act.activation(v_[par][:, c * COL:(c + 1) * COL], ps[:, c % 2, :], ACT.Copy)\
                        .then_inc(v_r, 1)

                def step(n, par, before, here, after):
                    if after:
                        square(n + 1, 0)
                        square(n + 1, 1)
                    if before:
                        exponent(n - 1)
                    if after:
                        square(n + 1, 2)
                        square(n + 1, 3)
                    if here:
                        keys_on(n)
                        for r in range(4):
                            turned(n, r)
                    if before:
                        widen(n - 1)
                        outputs(n - 1, 0)
                        outputs(n - 1, 1)
                    if after:
                        values(n + 1, 1 - par, 0)
                        values(n + 1, 1 - par, 1)

                step(-1, 1, False, False, True)
                step(0, 0, False, True, True)
                with act.Fori(0, NT // 2 - 1) as j:
                    step(2 * j + 1, 1, True, True, True)
                    step(2 * j + 2, 0, True, True, True)
                step(NT - 1, 1, True, True, False)
                step(NT, 0, True, False, False)

                act.wait_ge(y_r, NT * (l + 1) + 1)
                hold(act, lf, 16 * (l + 1))
                with act.Fori(0, NB) as b:
                    v = l * NB + b + 1
                    for u in U:
                        act.wait_ge(LN["nf"]["tr"][u], v)
                        act.activation(tf["xs"][u][0:64, :], Y[0:64, ds(seq_col(b, COL * u), COL)], ACT.Copy)\
                            .then_inc(xlo[u], 1)
                    for u in U:
                        act.wait_ge(LN["nf"]["tb"][u], v)
                        act.activation(tf["xn"][u], ps[:, bank[u][1], :], ACT.Identity,
                                       bias=WF[:, F_B:F_B + 1], scale=WF[:, F_G:F_G + 1]).then_inc(xn_r[u], 1)
                    for m in range(MF):
                        for u in U:
                            act.wait_ge(ag_mm[u], 2 * MF * (v - 1) + 2 * m + 1)
                            act.wait_ge(hf_r[u], MF * (v - 1) + m + 1)
                            act.activation(gf[u][0:FW[m], :], ps[0:FW[m], bank[u][(2 + 2 * m) % 4], :],
                                           ACT.Gelu, bias=WF[0:FW[m], F_BG + m:F_BG + m + 1])\
                                .then_inc(gate_r[u], 1)

        @block.vector
        def _(dve):
            dve.wait_ge(loaded, 64)

            def pre_norm(k):
                with dve.Fori(0, NB) as b:
                    v = k * NB + b + 1
                    for u in U:
                        kc = keep[:, ds(b * SEQ + COL * u, COL)]
                        if k == 0:
                            dve.tensor_copy(ta["z"][u], kc).then_inc(LN["pre"]["z"][u], 1)
                        else:
                            dve.wait_ge(kept[u], b + 1)
                            dve.tensor_tensor(ta["z"][u], kc, X[:, ds(seq_col(b, COL * u), COL)], ALU.add)\
                                .then_inc(LN["pre"]["z"][u], 1)
                    for u in U:
                        ln_stats(dve, "pre", u, v, bank[u][0], EPS_PRE)
                    for u in U:
                        ln_aggr(dve, "pre", u, v, EPS_PRE)
                    for u in U:
                        ln_norm(dve, "pre", u, v, bank[u][0], ta["zn"][u])

            pre_norm(0)
            with dve.Fori(0, BLOCKS) as l:
                dve.wait_ge(la1, 16 * (l + 1))
                dve.tensor_scalar(bias1[:, 0:2], Wa1[:, A1_B:A1_B + 2], 1.0, None, ALU.add).then_inc(biased, 1)
                hold(dve, biased, l + 1)
                with dve.Fori(0, NB) as b:
                    it = l * NB + b
                    for u in U:
                        dve.wait_ge(kvq[u], it + 1)
                        dve.tensor_scalar(ta["mk"][u], ps[:, bank[u][0], :], Wa1[:, A1_B:A1_B + 1], 0.0,
                                          ALU.add, ALU.min).then_inc(mins[u], 1)
                        dve.tensor_scalar(ta["den"][u], ps[:, bank[u][1], :], Wa1[:, A1_B + 1:A1_B + 2], 0.0,
                                          ALU.add, ALU.min).then_inc(mins[u], 1)
                    for u in U:
                        dve.wait_ge(exps[u], 2 * it + 1)
                        dve.scalar_tensor_tensor(ta["K"][u], ps[:, bank[u][0], :], bias1[:, 0:1], ta["ek"][u],
                                                 ALU.add, ALU.max, accum_out=kvp[:, u, 0:1])\
                            .then_inc(vprep[u], 1)
                        dve.wait_ge(exps[u], 2 * it + 2)
                        dve.tensor_scalar(ta["Vb"][u], ta["Vb"][u], 1.0, 1.0, ALU.subtract, ALU.add)\
                            .then_inc(rounded[u], 1)
                    for u in U:
                        dve.wait_ge(rounded[u], it + 1)
                        dve.scalar_tensor_tensor(Qf[:, ds(b * SEQ + COL * u, COL)], ps[:, bank[u][1], :],
                                                 bias1[:, 1:2], ta["Vb"][u], ALU.add, ALU.max)
                    for u in U:
                        dve.wait_ge(vprep[u], it + 1 + 2 * NB * l)
                        dve.scalar_tensor_tensor(ta["z"][u], ps[:, bank[u][2], :], Wa1[:, A1_B + 2:A1_B + 3],
                                                 ta["K"][u], ALU.add, ALU.mult, accum_out=kvp[:, u, 1:2])\
                            .then_inc(kq_used[u], 1)
                    for u in U:
                        dve.wait_ge(kq_used[u], it + 2)
                    dve.tensor_tensor(kvs[:, ds(b, 1), :], kvp[:, 0:1, :], kvp[:, 1:2, :], ALU.add)\
                        .then_inc(ksum, 1)
                hold(dve, ksum, NB * (l + 1))
                with dve.Fori(0, NB) as b:
                    v = l * NB + b + 1
                    base = NB * (l + 1) + 2 * (v - 1)
                    for u in U:
                        dve.tensor_scalar(ta["den"][u], Qf[:, ds(b * SEQ + COL * u, COL)], kvs[:, ds(b, 1), 0],
                                          EPS_Z, ALU.mult, ALU.add).then_inc(vprep[u], 1)
                    for u in U:
                        dve.wait_ge(vprep[u], base + 1)
                        dve.reciprocal(ta["K"][u], ta["den"][u]).then_inc(vprep[u], 1)
                    for u in U:
                        dve.wait_ge(vprep[u], base + 2)
                        dve.scalar_tensor_tensor(ta["Vb"][u], Qf[:, ds(b * SEQ + COL * u, COL)],
                                                 kvs[:, ds(b, 1), 1], ta["K"][u], ALU.mult, ALU.mult)\
                            .then_inc(vready[u], 1)
                    for u in U:
                        dve.wait_ge(ga[u], v)
                        dve.tensor_tensor(ta["z"][u], ta["g"][u], X[:, ds(seq_col(b, COL * u), COL)], ALU.add)\
                            .then_inc(LN["n1"]["z"][u], 1)
                    for u in U:
                        ln_stats(dve, "n1", u, v, bank[u][1], EPS_A)
                    for u in U:
                        ln_aggr(dve, "n1", u, v, EPS_A)
                    for u in U:
                        ln_norm(dve, "n1", u, v, bank[u][1], ta["zn"][u])
                    for u in U:
                        dve.wait_ge(g2[u], v)
                        dve.tensor_tensor(ta["z"][u], ta["g"][u], ta["x1"][u], ALU.add)\
                            .then_inc(LN["n2"]["z"][u], 1)
                    for u in U:
                        ln_stats(dve, "n2", u, v, bank[u][0], EPS_A)
                    for u in U:
                        ln_aggr(dve, "n2", u, v, EPS_A)
                    for u in U:
                        ln_norm(dve, "n2", u, v, bank[u][0], ta["zn"][u])
            for u in U:
                dve.wait_ge(x_done[u], NB * (BLOCKS + 1) + 1)
            pre_norm(1)

            dve.wait_ge(consts, 8)
            with dve.Fori(0, LAYERS) as l:
                for u in U:
                    dve.wait_ge(x_done[u], NB * (BLOCKS + 2 + l) + 1)
                dve.wait_ge(lb, 16 * (l + 1))
                for i in range(4):
                    s = WB[:, B_SC + i * DH:B_SC + (i + 1) * DH].unsqueeze(1).to_broadcast([P, TS, DH])
                    dve.tensor_tensor(tables[:, i, :, :], rotary[:, i, :, :], s, ALU.mult).then_inc(tab_r, 1)
                dve.wait_ge(tab_r, 4 * (l + 1))

                def xs(n, par):
                    g = l * NT + n
                    c = tile_col(n)
                    if not isinstance(n, int) or n > 1:
                        dve.wait_ge(v_mm, 2 * (g - 1) + 1)
                    dve.tensor_copy(xs_[par][0:64, :], X[0:64, ds(c, P)]).then_inc(xs_r, 1)
                    dve.tensor_copy(xs_[par][64:P, :], X[64:P, ds(c - 1, P)]).then_inc(xs_r, 1)

                def rotate(n, par, c):
                    g = l * NT + n
                    hc = COL // DH
                    dve.wait_ge(sq_r, QKC * g + c + 1)
                    if c == 0:
                        if not isinstance(n, int) or n > 1:
                            dve.wait_ge(tr_mm, 4 * (g - 1))
                    o = 2 * (c // 2)
                    src = ps[:, c % 2, :].rearrange("p (h d) -> p h d", d=DH)
                    a = t1[par][:, c * COL:(c + 1) * COL].rearrange("p (h d) -> p h d", d=DH)
                    bdst = t2[:, c * COL:(c + 1) * COL].rearrange("p (h d) -> p h d", d=DH)
                    cos = tables[:, o, ds(n % TS, 1), :].to_broadcast([P, hc, DH])
                    dve.tensor_tensor(a, src, cos, ALU.mult)
                    if c == 0:
                        dve.wait_ge(add_r, QKC * g + 1)
                    for i in range(2):
                        here, there = slice(32 * i, 32 * i + 32), slice(32 - 32 * i, 64 - 32 * i)
                        sin = tables[:, o + 1, ds(n % TS, 1), here].to_broadcast([P, hc, 32])
                        k = dve.tensor_tensor(bdst[:, :, here], src[:, :, there], sin, ALU.mult)
                    k.then_inc(rot_r, 1)

                def sumsq(n):
                    g = l * NT + n
                    for c in range(QKC):
                        dve.wait_ge(sq_r, QKC * g + c + 1)
                        dve.tensor_reduce(ssq[:, 8 * c:8 * c + 8],
                                          sq[:, c * COL:(c + 1) * COL].rearrange("p (h d) -> p h d", d=DH),
                                          AX_X, ALU.add).then_inc(red_r, 1)
                    dve.wait_ge(red_r, QKC * (g + 1) + 1)
                    dve.tensor_scalar(ssc[:, 0:HEADS], ssq[:, 0:HEADS], NORM_MIN, QK_SCALE ** -2,
                                      ALU.max, ALU.mult).then_inc(ssc_r, 1)
                    dve.tensor_scalar(ssc[:, HEADS:], ssq[:, HEADS:], NORM_MIN, None, ALU.max).then_inc(ssc_r, 1)

                def unit(n, par):
                    g = l * NT + n
                    dve.wait_ge(rinv_r, g + 1)
                    dve.wait_ge(add_r, QKC * (g + 1) + 1)
                    t3 = t1[par].rearrange("p (h d) -> p h d", d=DH)
                    dve.tensor_tensor(t3, t3, rinv[:, :].unsqueeze(2).to_broadcast([P, 2 * HEADS, DH]),
                                      ALU.mult).then_inc(qk_r, 1)

                def masked(n):
                    g = l * NT + n
                    dve.wait_ge(s_mm, g + 2)
                    for a in range(2):
                        m = maskt[:, ds(n % TS, 1), :].to_broadcast([P, NP, 2 * WIN])
                        i = dve.tensor_tensor(sc.rearrange("p (a h k) -> p a h k", a=2, h=NP)[:, a],
                                              ps[:, 4 + a, :].rearrange("p (h k) -> p h k", h=NP), m, ALU.add)
                    i.then_inc(s_rd, 1)
                    dve.wait_ge(s_rd, g + 2)
                    dve.tensor_reduce(mx[:, :], sc.rearrange("p (h k) -> p h k", h=HEADS), AX_X, ALU.max)\
                        .then_inc(max_r, 1)

                def totals(n):
                    g = l * NT + n
                    dve.wait_ge(exp_r, g + 1)
                    dve.tensor_reduce(rs[:, :], pe_.rearrange("p (h k) -> p h k", h=HEADS), AX_X, ALU.add)\
                        .then_inc(sum_r, 1)
                    dve.wait_ge(sum_r, g + 1)
                    dve.reciprocal(rr[:, :], rs[:, :]).then_inc(rec_r, 1)

                def turn_probs(n):
                    g = l * NT + n
                    dve.wait_ge(p_r, g + 1)
                    dve.wait_ge(ptd_r, g + 1)
                    dve.transpose(pt, pe_).then_inc(pt_r, 1)

                def residual(n):
                    g = l * NT + n
                    c = tile_col(n)
                    dve.wait_ge(wo_r, g + 2)
                    dve.tensor_tensor(Y[:, ds(c, P)], ps[:, 6, 0:P], X[:, ds(c, P)], ALU.add).then_inc(y_r, 1)

                def step(n, par, before, here, after):
                    if after:
                        xs(n + 1, 1 - par)
                    if before:
                        masked(n - 1)
                    if after:
                        rotate(n + 1, 1 - par, 0)
                        rotate(n + 1, 1 - par, 1)
                    if before:
                        totals(n - 1)
                    if after:
                        rotate(n + 1, 1 - par, 2)
                        rotate(n + 1, 1 - par, 3)
                    if before:
                        turn_probs(n - 1)
                    if after:
                        sumsq(n + 1)
                        unit(n + 1, 1 - par)
                    if before:
                        residual(n - 1)

                step(-1, 1, False, False, True)
                step(0, 0, False, True, True)
                with dve.Fori(0, NT // 2 - 1) as j:
                    step(2 * j + 1, 1, True, True, True)
                    step(2 * j + 2, 0, True, True, True)
                step(NT - 1, 1, True, True, False)
                step(NT, 0, True, False, False)

                dve.wait_ge(lf, 16 * (l + 1))
                hold(dve, y_r, NT * (l + 1) + 1)
                with dve.Fori(0, NB) as b:
                    v = l * NB + b + 1
                    for u in U:
                        dve.wait_ge(LN["nf"]["tr"][u], v)
                        dve.tensor_copy(tf["xs"][u][64:P, :], Y[64:P, ds(seq_col(b, COL * u) - 1, COL)])\
                            .then_inc(xhi[u], 1)
                    for u in U:
                        ln_stats(dve, "nf", u, v, bank[u][0], EPS_F)
                    for u in U:
                        ln_aggr(dve, "nf", u, v, EPS_F)
                    for u in U:
                        ln_norm(dve, "nf", u, v, bank[u][0], tf["zn"][u])
                    for m in range(MF):
                        for u in U:
                            dve.wait_ge(gate_r[u], MF * (v - 1) + m + 1)
                            dve.wait_ge(ag_mm[u], 2 * MF * (v - 1) + 2 * m + 2)
                            dve.scalar_tensor_tensor(hf[u][0:FW[m], m, :],
                                                     ps[0:FW[m], bank[u][(3 + 2 * m) % 4], :],
                                                     WF[0:FW[m], F_BA + m:F_BA + m + 1], gf[u][0:FW[m], :],
                                                     ALU.add, ALU.mult).then_inc(hf_r[u], 1)
                    for u in U:
                        col = ds(seq_col(b, COL * u), COL)
                        dve.wait_ge(o_mm[u], v)
                        dve.scalar_tensor_tensor(X[:, col], ps[:, bank[u][0], :], WF[:, F_B2:F_B2 + 1],
                                                 Y[:, col], ALU.add, ALU.add).then_inc(x_done[u], 1)
            for u in U:
                dve.wait_ge(x_done[u], NB * (BLOCKS + 2 + LAYERS) + 1)
            with dve.Fori(0, NB) as b:
                dve.tensor_tensor(keep[:, ds(b * SEQ, SEQ)], keep[:, ds(b * SEQ, SEQ)],
                                  X[:, ds(seq_col(b, 0), SEQ)], ALU.add).then_inc(finals, 1)


def constant_tables():
    f = np.float32
    half = np.arange(0, DH, 2, dtype=f)
    inv = (f(1.0) / f(10000.0) ** (half / f(DH))).astype(f)
    t = np.arange(SEQ, dtype=f)
    fr = t[:, None] * inv[None, :]
    fr = np.concatenate([fr, fr], -1).astype(np.float64)
    base = ((half + f(0.4 * DH)) / f(1.4 * DH)).astype(f)
    power = (t - SEQ // 2) / (WIN // 2)
    scale = base[None, :].astype(np.float64) ** power[:, None]
    scale = np.concatenate([scale, scale], -1)
    sign = np.concatenate([-np.ones(DH // 2), np.ones(DH // 2)])
    cos, sin = np.cos(fr), np.sin(fr) * sign
    rot = np.stack([cos * scale, sin * scale, cos / scale, sin / scale]).astype(f)
    rot = rot.reshape(4, TS, P, DH).transpose(2, 0, 1, 3).reshape(P, 4 * TS * DH)
    i, j = np.arange(WIN)[:, None], np.arange(WIN)[None, :]
    before, own = np.where(i > j, NEG, 0.0), np.where(i < j, NEG, 0.0)
    mask = np.tile(np.concatenate([before, own], 1)[None, None], (TS, P // WIN, 1, 1))
    mask[0, 0, :, :WIN] = NEG
    mask = mask.reshape(TS, P, 2 * WIN).transpose(1, 0, 2).reshape(P, TS * 2 * WIN).astype(f)
    mask = np.concatenate([mask, np.tile((np.arange(TS) > 0).astype(f), (P, 1))], 1)
    return np.ascontiguousarray(rot), np.ascontiguousarray(mask)


def kernel(**inputs):
    import concourse.bacc as _bacc
    from concourse.bass_utils import run_bass_kernel_spmd as _run

    i = {k: np.asarray(v) for k, v in inputs.items()}
    A = {k[len("L0_attn_"):]: v for k, v in i.items() if k.startswith("L0_attn_")}
    B = {k[len("L0_ffn_"):]: v for k, v in i.items() if k.startswith("L0_ffn_")}

    def col(v):
        return v[:, :, None]

    def chunks(w, n, rows):
        full = np.zeros((w.shape[0], n * P, w.shape[2]), w.dtype)
        full[:, :rows] = w
        return full.reshape(w.shape[0], n, P, -1).transpose(0, 2, 1, 3).reshape(w.shape[0], P, -1)

    wa1 = np.concatenate([A["Wq"], A["Wk"], A["Wv"], col(A["bk"]), col(A["bq"]), col(A["bv"])], 2)
    wa2 = np.concatenate([A["Wo"], A["Wf1"], chunks(A["Wf2"], MA, FA), col(A["bo"]), col(A["ln1_s"]),
                          col(A["ln1_b"]), chunks(col(A["bf1"]), MA, FA), col(A["bf2"]), col(A["ln2_s"]),
                          col(A["ln2_b"])], 2)

    def spread(v):
        return np.broadcast_to(v[:, None, :], (LAYERS, P, DH))

    def swap(v):
        return np.concatenate([v[:, DH // 2:], v[:, :DH // 2]], 1)

    qs, ks = B["q_scale"], B["k_scale"]
    wb = np.concatenate([B["Wqkv"], chunks(B["Wo"], NP, INNER), spread(qs), spread(swap(qs)), spread(ks),
                         spread(swap(ks))], 2)
    wf = np.concatenate([B["W1"], chunks(B["W2"], MF, HID), col(B["ln_g"]), col(B["ln_b"]),
                         chunks(col(B["b1"][:, :HID]), MF, HID), chunks(col(B["b1"][:, HID:]), MF, HID),
                         col(B["b2"])], 2)
    rot, mask = constant_tables()
    arrays = {"xT": A["x"].reshape(NB * SEQ, D).T, "wa1": wa1.reshape(-1, A1_W), "wa2": wa2.reshape(-1, A2_W),
              "wb": wb.reshape(-1, B_W), "wf": wf.reshape(-1, F_W), "rot": rot, "mask": mask}
    arrays = {k: np.ascontiguousarray(v) for k, v in arrays.items()}
    nc = _bacc.Bacc("TRN2", target_bir_lowering=False, num_devices=1)
    args = [nc.dram_tensor(k, v.shape, F32, kind="ExternalInput").ap() for k, v in arrays.items()]
    out = nc.dram_tensor("outT", [D, NB * SEQ], F32, kind="ExternalOutput").ap()
    build(nc, *args, out)
    r = _run(nc, [arrays], core_ids=[0])
    return np.ascontiguousarray(r.results[0]["outT"].T).reshape(NB, SEQ, D)
```

```python
from contextlib import ExitStack

import numpy as np
import concourse.bass as bass
from concourse import mybir

F32 = mybir.dt.float32
I32 = mybir.dt.int32
ALU = mybir.AluOpType
ACT = mybir.ActivationFunctionType
AX_X = mybir.AxisListType.X
ds = bass.ds

P = 128
NB, SEQ, D = 4, 1024, 128
BLOCKS, FA = 8, 512
MA = FA // P
LAYERS, HEADS, DH, WIN = 6, 16, 64, 32
INNER = HEADS * DH
HID = int(D * 4 * 2 / 3)
MF = -(-HID // P)
FW = [min(P, HID - P * m) for m in range(MF)]
COL = 512
UT = SEQ // COL
TS = SEQ // P
NT = NB * TS
SP1 = SEQ + 1
NP = HEADS // 2
QKC = 2 * INNER // COL
RING = 3
HEAD, TAIL = range(-1, 3), range(NT - 2, NT + 3)
NEG = -1.0e30
EPS_PRE, EPS_A, EPS_F, EPS_Z = 1e-5, 1e-6, 1e-5, 1e-6
NORM_MIN = 1e-24
QK_SCALE = 8.0
ROOT_BITS = 1597463007.0
NEWTON = 3

A1_B = 3 * D
A1_W = A1_B + 3
A2_F1, A2_F2 = D, D + FA
A2_V = A2_F2 + MA * D
A2_BO, A2_S1, A2_B1, A2_BF1 = A2_V, A2_V + 1, A2_V + 2, A2_V + 3
A2_BF2 = A2_BF1 + MA
A2_S2, A2_B2 = A2_BF2 + 1, A2_BF2 + 2
A2_W = A2_B2 + 1
B_WO = 3 * INNER
B_SC = B_WO + NP * D
B_W = B_SC + 4 * DH
F_W2 = 2 * HID
F_G = F_W2 + MF * D
F_B = F_G + 1
F_BA = F_B + 1
F_BG = F_BA + MF
F_B2 = F_BG + MF
F_W = F_B2 + 1


def build(nc, xT, wa1, wa2, wb, wf, rot, mask, outT):
    with ExitStack() as ctx:
        def sb(name, shape):
            return ctx.enter_context(nc.sbuf_tensor(name, shape, F32))

        def sem(name):
            return ctx.enter_context(nc.semaphore(name))

        def pair(name):
            return [sem(f"{name}_{u}") for u in range(UT)]

        ps = ctx.enter_context(nc.psum_tensor("ps", [P, 8, COL], F32))

        X = sb("X", [P, NB * SP1])
        Y = sb("Y", [P, NB * SP1])
        keep = sb("keep", [P, NB * SEQ])
        ident = sb("ident", [P, P])
        power = sb("power", [P, 4])
        WB = sb("WB", [P, B_W])
        WF = sb("WF", [P, F_W])
        rotary = sb("rotary", [P, 4, TS, DH])
        tables = sb("tables", [P, 4, TS, DH])
        maskt = sb("maskt", [P, TS, 2 * WIN])
        inside = sb("inside", [P, TS])
        stats = sb("stats", [P, UT, 4, 6])
        mv = sb("mv", [P, UT, 4, 2])
        ve = sb("ve", [P, UT, 4])
        rstd = sb("rstd", [P, UT, 4])
        kvp = sb("kvp", [P, UT, 2])
        kvs = sb("kvs", [P, NB, 2])
        bias1 = sb("bias1", [P, 3])
        ssq = sb("ssq", [P, 2 * HEADS])
        ssc = sb("ssc", [P, 2 * HEADS])
        nwt = sb("nwt", [P, 2, 2 * HEADS])
        rinv = sb("rinv", [P, 2 * HEADS])
        mx = sb("mx", [P, HEADS])
        rs = sb("rs", [P, HEADS])
        rr = sb("rr", [P, HEADS])

        arena = sb("arena", [P, 24600])

        def carve(sizes):
            at, got = 0, []
            for n in sizes:
                got.append(arena[:, at:at + n])
                at += n
            return got

        (Wa1, Wa2, Qf, *rest) = carve([A1_W, A2_W, NB * SEQ] + [COL] * (UT * 13))
        ta = {k: [rest[i * UT + u] for u in range(UT)]
              for i, k in enumerate(["mk", "ek", "K", "den", "Vb", "g", "z", "zn", "x1"])}
        ha = [arena[:, A1_W + A2_W + NB * SEQ + COL * (18 + MA * u):][:, 0:MA * COL]
              .rearrange("p (m n) -> p m n", m=MA) for u in range(UT)]
        (t1, t2, sq, sc, pe_, pt, PTd, qTf, kTf, OTf, *rings) = carve(
            [2 * INNER] * 3 + [INNER] * 3 + [2 * HEADS * P] + [INNER] + [NP * (WIN + P)] + [INNER]
            + [INNER] * (2 * RING) + [P] * RING)
        v_, vs_, xs_ = rings[:RING], rings[RING:2 * RING], rings[2 * RING:]
        qT = qTf.rearrange("p (c t) -> p c t", c=NP)
        kT = kTf.rearrange("p (c t) -> p c t", c=NP)
        OT = OTf.rearrange("p (c t) -> p c t", c=NP)
        fa = arena[:, 0:7 * INNER].rearrange("p (k n) -> p k n", n=COL)
        tf = {k: [fa[:, i * UT + u, :] for u in range(UT)] for i, k in enumerate(["xs", "zn", "xn"])}
        gf = [fa[:, 6 + u, :] for u in range(UT)]
        hf = [fa[:, 8 + MF * u:8 + MF * u + MF, :] for u in range(UT)]

        loaded, consts = sem("loaded"), sem("consts")
        la1, la2, lb, lf = sem("wa1_in"), sem("wa2_in"), sem("wb_in"), sem("wf_in")
        stored = sem("stored")
        x_done = pair("x_done")

        LN = {k: {s: pair(f"{k}_{s}") for s in ("z", "tr", "stat", "rstd", "zn", "tb")}
              for k in ("pre", "n1", "n2", "nf")}
        xlo, xhi = pair("xs_lo"), LN["nf"]["z"]
        kept = pair("kept")
        kvq, mins, exps, kq_used = pair("kvq_mm"), pair("mins"), pair("exps"), pair("kvq_used")
        rounded = pair("q_rounded")
        ksum = sem("seq_sums")
        biased = sem("bias1_ready")
        vprep, vready, wo_mm, ga = pair("v_chain"), pair("v_ready"), pair("wo_mm"), pair("attn_gelu")
        x1_r, f1_mm, h_r, f2_mm, g2 = pair("x1_r"), pair("f1_mm"), pair("h_r"), pair("f2_mm"), pair("ff_gelu")

        xn_r, ag_mm, gate_r, hf_r, o_mm = map(pair, ("xn_r", "ag_mm", "gate_r", "hf_r", "o_mm"))
        finals, passed = sem("finals"), sem("waits_passed")

        (tab_r, xs_r, qk_mm, v_mm, sq_r, rot_r, add_r, red_r, ssc_r, newton, qk_r, tr_mm, shift_r, tr_ev,
         s_mm, s_rd, max_r, sub_r, exp_r, sum_r, rec_r, p_r, pt_r, ptd_r, pv_mm, ot_r, wo_r, y_r, v_r,
         vs_in) = map(sem, (
             "tables_ready", "xs_ready", "qk_mm", "v_mm", "squares", "rotated", "added", "sumsq",
             "sumsq_clamped", "newton", "qk_ready", "transposed", "keys_shifted", "transposes_out",
             "scores_mm", "scores_masked", "max_ready", "shifted", "exp_ready", "sum_ready", "recip_ready",
             "probs_ready", "probsT_ready", "probsT_wide", "pv_mm", "ot_ready", "wo_done", "y_ready",
             "v_ready_b", "vshift_in"))

        def seq_col(b, t):
            return b * SP1 + 1 + t

        def tile_col(n):
            return n * P + n // TS + 1

        def hold(eng, s, v):
            eng.wait_ge(s, v)
            eng.sem_inc(passed, 1)

        def live(n):
            return not isinstance(n, int) or 0 <= n < NT

        def walk(eng, step):
            for n in HEAD:
                step(n, n % RING)
            with eng.Fori(0, (TAIL[0] - HEAD[-1] - 1) // RING) as j:
                for i in range(RING):
                    step(RING * j + HEAD[-1] + 1 + i, (HEAD[-1] + 1 + i) % RING)
            for n in TAIL:
                step(n, n % RING)

        def c4(ap):
            return ap.rearrange("p (j t) -> p j t", j=4)

        def ln_turn(pe, k, u, v, src, bank):
            pe.wait_ge(LN[k]["z"][u], v)
            for j in range(4):
                i = pe.transpose(ps[:, bank, j * P:(j + 1) * P], src[:, j * P:(j + 1) * P], ident[:, :])
            i.then_inc(LN[k]["tr"][u], 1)

        def ln_stats(dve, k, u, v, bank, eps):
            st = LN[k]["stat"][u]
            dve.wait_ge(LN[k]["tr"][u], v + 1)
            for j in range(4):
                i = dve.bn_stats(stats[:, u, j, :], ps[:, bank, j * P:(j + 1) * P])
            i.then_inc(st, 1)

        def ln_aggr(dve, k, u, v, eps):
            st = LN[k]["stat"][u]
            hold(dve, st, 3 * v - 2)
            for j in range(4):
                i = dve.bn_aggr(mv[:, u, j, :], stats[:, u, j, :])
            i.then_inc(st, 1)
            dve.wait_ge(st, 3 * v - 1)
            dve.tensor_scalar(ve[:, u, :], mv[:, u, :, 1], eps, None, ALU.add).then_inc(st, 1)

        def ln_rstd(pool, k, u, v):
            pool.wait_ge(LN[k]["stat"][u], 3 * v)
            pool.tensor_tensor(rstd[:, u, :], ve[:, u, :], power[:, 0:4], ALU.pow)\
                .then_inc(LN[k]["rstd"][u], 1)

        def ln_norm(dve, k, u, v, bank, dst):
            dve.wait_ge(LN[k]["rstd"][u], v)
            for j in range(4):
                i = dve.tensor_scalar(dst[:, j * P:(j + 1) * P], ps[:, bank, j * P:(j + 1) * P],
                                      mv[:, u, j, 0:1], rstd[:, u, j:j + 1], ALU.subtract, ALU.mult)
            i.then_inc(LN[k]["zn"][u], 1)

        def ln_back(pe, k, u, v, src, bank):
            pe.wait_ge(LN[k]["zn"][u], v)
            for j in range(4):
                i = pe.transpose(ps[:, bank, j * P:(j + 1) * P], src[:, j * P:(j + 1) * P], ident[:, :])
            i.then_inc(LN[k]["tb"][u], 1)

        U = range(UT)
        bank = [[4 * u + i for i in range(4)] for u in U]
        block = ctx.enter_context(nc.Block())

        @block.sync
        def _(sp):
            for s in (v_mm, tr_mm, wo_r, v_r, s_rd, y_r, ptd_r, red_r, s_mm, pt_r, pv_mm, vs_in, add_r,
                      *kq_used, *hf_r, *kept, *x_done, *(q for k in LN.values() for q in k["tr"])):
                sp.sem_inc(s, 1)
            sp.dma_start(keep[:, :], xT).then_inc(loaded, 16)
            sp.dma_start(rotary[:, :, :, :].rearrange("p a b c -> p (a b c)"), rot).then_inc(loaded, 16)
            sp.dma_start(maskt[:, :, :].rearrange("p a b -> p (a b)"), mask[:, 0:TS * 2 * WIN]).then_inc(loaded, 16)
            sp.dma_start(inside[:, :], mask[:, TS * 2 * WIN:]).then_inc(loaded, 16)
            with sp.Fori(0, BLOCKS) as l:
                for u in U:
                    hold(sp, kq_used[u], NB * l + 1)
                sp.dma_start(Wa1, wa1[ds(l * P, P), :]).then_inc(la1, 16)
                for u in U:
                    hold(sp, x_done[u], NB * (l + 1) + 1)
                sp.dma_start(Wa2, wa2[ds(l * P, P), :]).then_inc(la2, 16)
            with sp.Fori(0, LAYERS) as l:
                hold(sp, v_mm, NT * 2 * l + 1)
                hold(sp, wo_r, NT * l + 1)
                sp.dma_start(WB[:, :], wb[ds(l * P, P), :]).then_inc(lb, 16)
                for u in U:
                    hold(sp, x_done[u], NB * (BLOCKS + 2 + l) + 1)
                sp.dma_start(WF[:, :], wf[ds(l * P, P), :]).then_inc(lf, 16)

                def vshift(n, r):
                    if not live(n):
                        return
                    g = l * NT + n
                    hold(sp, v_r, 2 * g + 3)
                    sp.dma_start(vs_[r][WIN:P, :], v_[r][0:P - WIN, :]).then_inc(vs_in, 16)
                    sp.dma_start(vs_[r][0:WIN, :], v_[r - 1][P - WIN:P, :]).then_inc(vs_in, 16)

                walk(sp, vshift)
            sp.wait_ge(finals, NB)
            sp.dma_start(outT, keep[:, :]).then_inc(stored, 16)
            sp.wait_ge(stored, 16)

        @block.gpsimd
        def _(pool):
            pool.memset(ident[:, :], 0.0).then_inc(consts, 1)
            pool.memset(power[:, :], -0.5).then_inc(consts, 1)
            pool.wait_ge(consts, 1)
            pool.affine_select(out=ident[:, :], in_=ident[:, :], compare_op=ALU.not_equal, fill=1.0, base=0,
                               pattern=[[-1, P]], channel_multiplier=1).then_inc(consts, 1)
            pool.memset(X[:, :], 0.0).then_inc(consts, 1)
            pool.memset(Y[:, :], 0.0).then_inc(consts, 1)
            pool.wait_ge(consts, 5)

            def pre_norm(k):
                with pool.Fori(0, NB) as b:
                    for u in U:
                        ln_rstd(pool, "pre", u, k * NB + b + 1)

            pre_norm(0)
            with pool.Fori(0, BLOCKS) as l:
                with pool.Fori(0, NB) as b:
                    for k in ("n1", "n2"):
                        for u in U:
                            ln_rstd(pool, k, u, l * NB + b + 1)
            pre_norm(1)
            for u in U:
                pool.wait_ge(x_done[u], NB * (BLOCKS + 2) + 1)
            pool.memset(PTd, 0.0).then_inc(consts, 1)
            pool.memset(kTf, 0.0).then_inc(consts, 1)
            pool.memset(v_[RING - 1], 0.0).then_inc(consts, 1)
            with pool.Fori(0, LAYERS) as l:
                def probs_sub(n):
                    g = l * NT + n
                    pool.wait_ge(max_r, g + 1)
                    s3 = sc.rearrange("p (h k) -> p h k", h=HEADS)
                    pool.tensor_tensor(s3, s3, mx[:, :].unsqueeze(2).to_broadcast([P, HEADS, 2 * WIN]),
                                       ALU.subtract).then_inc(sub_r, 1)

                def probs_norm(n):
                    g = l * NT + n
                    pool.wait_ge(rec_r, g + 1)
                    p3 = pe_.rearrange("p (h k) -> p h k", h=HEADS)
                    pool.tensor_tensor(p3, p3, rr[:, :].unsqueeze(2).to_broadcast([P, HEADS, 2 * WIN]),
                                       ALU.mult).then_inc(p_r, 1)

                def add(n, c):
                    g = l * NT + n
                    pool.wait_ge(rot_r, QKC * g + c + 1)
                    w = slice(c * COL, (c + 1) * COL)
                    pool.tensor_tensor(t1[:, w], t1[:, w], t2[:, w], ALU.add).then_inc(add_r, 1)

                def step(n, r):
                    if live(n - 1):
                        probs_sub(n - 1)
                    if live(n + 1):
                        add(n + 1, 0)
                        add(n + 1, 1)
                    if live(n - 1):
                        probs_norm(n - 1)
                    if live(n + 1):
                        add(n + 1, 2)
                        add(n + 1, 3)

                walk(pool, step)
                with pool.Fori(0, NB) as b:
                    for u in U:
                        ln_rstd(pool, "nf", u, l * NB + b + 1)

        @block.tensor
        def _(pe):
            pe.wait_ge(consts, 3)

            def pre_norm(k):
                with pe.Fori(0, NB) as b:
                    v = k * NB + b + 1
                    for u in U:
                        ln_turn(pe, "pre", u, v, ta["z"][u], bank[u][0])
                    for u in U:
                        pe.wait_ge(x_done[u], k * NB * (BLOCKS + 1) + b + 1)
                        ln_back(pe, "pre", u, v, ta["zn"][u], bank[u][1])

            pre_norm(0)
            with pe.Fori(0, BLOCKS) as l:
                pe.wait_ge(la1, 16 * (l + 1))
                for u in U:
                    hold(pe, x_done[u], NB * (l + 1) + 1)
                with pe.Fori(0, NB) as b:
                    it = l * NB + b
                    for u in U:
                        pe.wait_ge(kq_used[u], it + 1)
                        xcol = X[:, ds(seq_col(b, COL * u), COL)]
                        for i, w in enumerate((1, 0, 2)):
                            m = pe.matmul(ps[:, bank[u][i], :], Wa1[:, w * D:(w + 1) * D], xcol,
                                          start=True, stop=True)
                        m.then_inc(kvq[u], 1)
                hold(pe, la2, 16 * (l + 1))
                with pe.Fori(0, NB) as b:
                    v = l * NB + b + 1
                    for u in U:
                        pe.wait_ge(vready[u], v)
                        pe.matmul(ps[:, bank[u][0], :], Wa2[:, 0:D], ta["Vb"][u], start=True, stop=True)\
                            .then_inc(wo_mm[u], 1)
                    for u in U:
                        ln_turn(pe, "n1", u, v, ta["z"][u], bank[u][1])
                    for u in U:
                        ln_back(pe, "n1", u, v, ta["zn"][u], bank[u][2])
                    for u in U:
                        pe.wait_ge(x1_r[u], v)
                        for m in range(MA):
                            pe.matmul(ps[:, bank[u][(3 + m) % 4], :], Wa2[:, A2_F1 + m * P:A2_F1 + (m + 1) * P],
                                      ta["x1"][u], start=True, stop=True).then_inc(f1_mm[u], 1)
                    for u in U:
                        for m in range(MA):
                            pe.wait_ge(h_r[u], MA * (v - 1) + m + 1)
                            i = pe.matmul(ps[:, bank[u][3], :], Wa2[:, A2_F2 + m * D:A2_F2 + (m + 1) * D],
                                          ha[u][:, m, :], start=(m == 0), stop=(m == MA - 1))
                        i.then_inc(f2_mm[u], 1)
                    for u in U:
                        ln_turn(pe, "n2", u, v, ta["z"][u], bank[u][0])
                    for u in U:
                        ln_back(pe, "n2", u, v, ta["zn"][u], bank[u][1])
            pre_norm(1)

            pe.wait_ge(consts, 8)
            with pe.Fori(0, LAYERS) as l:
                def project(n, r, c):
                    g = l * NT + n
                    if c == 0:
                        pe.wait_ge(xs_r, 2 * g + 2)
                    if c < 2:
                        pe.wait_ge(v_r, 2 * g + c)
                    else:
                        pe.wait_ge(rot_r, QKC * g + c - 1)
                    pe.matmul(ps[:, c % 2, :], xs_[r], WB[:, c * COL:(c + 1) * COL], start=True,
                              stop=True).then_inc(qk_mm if c < QKC else v_mm, 1)

                def turn(n):
                    g = l * NT + n
                    pe.wait_ge(qk_r, g + 1)
                    for r in range(4):
                        if r >= 2:
                            pe.wait_ge(tr_ev, 4 * g + r - 1)
                        for j in range(4):
                            c = 4 * r + j
                            i = pe.transpose(ps[:, 2 + r % 2, j * P:(j + 1) * P],
                                             t1[:, c * P:(c + 1) * P], ident[:, :])
                        i.then_inc(tr_mm, 1)

                def scores(n):
                    g = l * NT + n
                    pe.wait_ge(s_rd, g + 1)
                    hold(pe, tr_ev, 4 * g + 4)
                    for w in range(4):
                        for h in range(HEADS):
                            r = 64 * (h % 2)
                            i = pe.matmul(ps[WIN * w:WIN * (w + 1), 4 + h % 2, (h // 2) * 64:(h // 2) * 64 + 64],
                                          qT[r:r + 64, h // 2, WIN * w:WIN * (w + 1)],
                                          kT[r:r + 64, h // 2, WIN * w:WIN * (w + 2)], start=True, stop=True)
                    i.then_inc(s_mm, 1)

                def attend(n, r, half):
                    g = l * NT + n
                    if half == 0:
                        pe.wait_ge(ptd_r, g + 2)
                        pe.wait_ge(vs_in, 32 * (g + 1) + 1)
                        pe.wait_ge(y_r, g + 1)
                    pw = PTd.rearrange("p (a c k q) -> p a c k q", a=2, c=NP, k=2)
                    for c in range(4 * half, 4 * half + 4):
                        for part, val in ((1, v_[r]), (0, vs_[r])):
                            for a in range(2):
                                h = 2 * c + a
                                i = pe.matmul(ps[64 * a:64 * a + 64, 6 + half, (c % 4) * P:(c % 4 + 1) * P],
                                              val[:, h * DH:(h + 1) * DH], pw[:, a, c, part, :],
                                              start=(part == 1), stop=(part == 0))
                    i.then_inc(pv_mm, 1)

                def output(n):
                    g = l * NT + n
                    for c in range(NP):
                        if c % 4 == 0:
                            pe.wait_ge(ot_r, 2 * g + 1 + c // 4)
                        i = pe.matmul(ps[:, 6, 0:P], WB[:, B_WO + c * D:B_WO + (c + 1) * D], OT[:, c, :],
                                      start=(c == 0), stop=(c == NP - 1))
                    i.then_inc(wo_r, 1)

                def step(n, r):
                    new, old = (r + 1) % RING, (r - 2) % RING
                    if live(n):
                        turn(n)
                    if live(n + 1):
                        project(n + 1, new, 0)
                        project(n + 1, new, 1)
                    if live(n - 2):
                        attend(n - 2, old, 0)
                    if live(n + 1):
                        project(n + 1, new, 2)
                        project(n + 1, new, 3)
                    if live(n - 2):
                        attend(n - 2, old, 1)
                    if live(n):
                        scores(n)
                    if live(n - 2):
                        output(n - 2)
                    if live(n + 1):
                        project(n + 1, new, 4)
                        project(n + 1, new, 5)

                pe.wait_ge(lb, 16 * (l + 1))
                walk(pe, step)

                hold(pe, lf, 16 * (l + 1))
                with pe.Fori(0, NB) as b:
                    v = l * NB + b + 1
                    for u in U:
                        pe.wait_ge(xlo[u], v)
                        ln_turn(pe, "nf", u, v, tf["xs"][u], bank[u][0])
                    for u in U:
                        ln_back(pe, "nf", u, v, tf["zn"][u], bank[u][1])
                    for m in range(MF):
                        for u in U:
                            if m == 0:
                                pe.wait_ge(xn_r[u], v)
                            if m == 2:
                                pe.wait_ge(hf_r[u], MF * (v - 1) + 2)
                            for k in (1, 0):
                                pe.matmul(ps[0:FW[m], bank[u][(2 + 2 * m + 1 - k) % 4], :],
                                          WF[:, k * HID + m * P:k * HID + m * P + FW[m]], tf["xn"][u],
                                          start=True, stop=True).then_inc(ag_mm[u], 1)
                    for u in U:
                        for m in range(MF):
                            if m == 0:
                                pe.wait_ge(hf_r[u], MF * (v - 1) + 2 + 1)
                            elif m == 2:
                                pe.wait_ge(hf_r[u], MF * v + 1)
                            i = pe.matmul(ps[:, bank[u][0], :], WF[0:FW[m], F_W2 + m * D:F_W2 + (m + 1) * D],
                                          hf[u][0:FW[m], m, :], start=(m == 0), stop=(m == MF - 1))
                        i.then_inc(o_mm[u], 1)

        @block.scalar
        def _(act):
            def pre_norm(k):
                with act.Fori(0, NB) as b:
                    v = k * NB + b + 1
                    for u in U:
                        if k:
                            act.wait_ge(LN["pre"]["z"][u], v)
                            act.activation(keep[:, ds(b * SEQ + COL * u, COL)], ta["z"][u], ACT.Copy)\
                                .then_inc(kept[u], 1)
                    for u in U:
                        act.wait_ge(LN["pre"]["tb"][u], v)
                        act.activation(X[:, ds(seq_col(b, COL * u), COL)], ps[:, bank[u][1], :], ACT.Copy)\
                            .then_inc(x_done[u], 1)

            act.wait_ge(consts, 5)
            pre_norm(0)
            with act.Fori(0, BLOCKS) as l:
                with act.Fori(0, NB) as b:
                    v = l * NB + b + 1
                    for u in U:
                        for i, k in enumerate(("ek", "K")):
                            act.wait_ge(mins[u], 2 * v - 1 + i)
                            src = ta["mk"][u] if i == 0 else ta["den"][u]
                            act.activation(ta["ek"][u] if i == 0 else ta["Vb"][u], src, ACT.Exp)\
                                .then_inc(exps[u], 1)
                hold(act, la2, 16 * (l + 1))
                with act.Fori(0, NB) as b:
                    v = l * NB + b + 1
                    for u in U:
                        act.wait_ge(wo_mm[u], v)
                        act.activation(ta["g"][u], ps[:, bank[u][0], :], ACT.Gelu_apprx_tanh,
                                       bias=Wa2[:, A2_BO:A2_BO + 1]).then_inc(ga[u], 1)
                    for u in U:
                        act.wait_ge(LN["n1"]["tb"][u], v)
                        act.activation(ta["x1"][u], ps[:, bank[u][2], :], ACT.Identity,
                                       bias=Wa2[:, A2_B1:A2_B1 + 1], scale=Wa2[:, A2_S1:A2_S1 + 1])\
                            .then_inc(x1_r[u], 1)
                    for u in U:
                        for m in range(MA):
                            act.wait_ge(f1_mm[u], MA * (v - 1) + m + 1)
                            act.activation(ha[u][:, m, :], ps[:, bank[u][(3 + m) % 4], :], ACT.Gelu_apprx_tanh,
                                           bias=Wa2[:, A2_BF1 + m:A2_BF1 + m + 1]).then_inc(h_r[u], 1)
                    for u in U:
                        act.wait_ge(f2_mm[u], v)
                        act.activation(ta["g"][u], ps[:, bank[u][3], :], ACT.Gelu_apprx_tanh,
                                       bias=Wa2[:, A2_BF2:A2_BF2 + 1]).then_inc(g2[u], 1)
                    for u in U:
                        act.wait_ge(LN["n2"]["tb"][u], v)
                        act.activation(X[:, ds(seq_col(b, COL * u), COL)], ps[:, bank[u][1], :], ACT.Identity,
                                       bias=Wa2[:, A2_B2:A2_B2 + 1], scale=Wa2[:, A2_S2:A2_S2 + 1])\
                            .then_inc(x_done[u], 1)
            pre_norm(1)

            act.wait_ge(consts, 8)
            act.wait_ge(loaded, 64)
            with act.Fori(0, LAYERS) as l:
                def square(n, c):
                    g = l * NT + n
                    act.wait_ge(qk_mm, QKC * g + c + 1)
                    if c == 0:
                        act.wait_ge(red_r, QKC * g + 1)
                    act.activation(sq[:, c * COL:(c + 1) * COL], ps[:, c % 2, :], ACT.Square)\
                        .then_inc(sq_r, 1)

                def keys_on(n):
                    g = l * NT + n
                    act.wait_ge(s_mm, g + 1)
                    act.activation(kT[:, :, 0:WIN], kT[:, :, P:P + WIN], ACT.Copy,
                                   scale=inside[:, ds(n % TS, 1)]).then_inc(shift_r, 1)
                    act.wait_ge(shift_r, g + 1)

                def turned(n, r):
                    g = l * NT + n
                    act.wait_ge(tr_mm, 4 * g + r + 2)
                    dst = (qT[:, 4 * r:4 * r + 4, :] if r < 2 else
                           kT[:, 4 * (r - 2):4 * (r - 2) + 4, WIN:WIN + P])
                    act.activation(dst, c4(ps[:, 2 + r % 2, :]), ACT.Copy).then_inc(tr_ev, 1)

                def exponent(n):
                    g = l * NT + n
                    act.wait_ge(sub_r, g + 1)
                    act.wait_ge(pt_r, g + 1)
                    act.activation(pe_, sc, ACT.Exp).then_inc(exp_r, 1)

                def widen(n):
                    g = l * NT + n
                    act.wait_ge(pt_r, g + 2)
                    act.wait_ge(pv_mm, 2 * g + 1)
                    for w in range(4):
                        q = slice(WIN * w, WIN * (w + 1))
                        i = act.activation(PTd.rearrange("p (k q) -> p k q", q=P)[q, :, q],
                                           pt.rearrange("p (k q) -> p k q", q=WIN)[q, :, :], ACT.Copy)
                    i.then_inc(ptd_r, 1)

                def outputs(n, r):
                    g = l * NT + n
                    act.wait_ge(pv_mm, 2 * g + 1 + r + 1)
                    if r == 0:
                        act.wait_ge(wo_r, g + 1)
                    act.activation(OT[:, 4 * r:4 * r + 4, :], c4(ps[:, 6 + r, :]), ACT.Copy).then_inc(ot_r, 1)

                def values(n, r, c):
                    g = l * NT + n
                    act.wait_ge(v_mm, 2 * g + c + 2)
                    if c == 0:
                        act.wait_ge(vs_in, 32 * g + 1)
                    act.activation(v_[r][:, c * COL:(c + 1) * COL], ps[:, c % 2, :], ACT.Copy)\
                        .then_inc(v_r, 1)

                def step(n, r):
                    if live(n):
                        keys_on(n)
                        for q in range(4):
                            turned(n, q)
                    if live(n + 1):
                        square(n + 1, 0)
                        square(n + 1, 1)
                    if live(n - 1):
                        exponent(n - 1)
                    if live(n - 2):
                        outputs(n - 2, 0)
                    if live(n + 1):
                        square(n + 1, 2)
                        square(n + 1, 3)
                    if live(n - 2):
                        outputs(n - 2, 1)
                    if live(n - 1):
                        widen(n - 1)
                    if live(n + 1):
                        values(n + 1, (r + 1) % RING, 0)
                        values(n + 1, (r + 1) % RING, 1)

                walk(act, step)

                act.wait_ge(y_r, NT * (l + 1) + 1)
                hold(act, lf, 16 * (l + 1))
                with act.Fori(0, NB) as b:
                    v = l * NB + b + 1
                    for u in U:
                        act.wait_ge(LN["nf"]["tr"][u], v)
                        act.activation(tf["xs"][u][0:64, :], Y[0:64, ds(seq_col(b, COL * u), COL)], ACT.Copy)\
                            .then_inc(xlo[u], 1)
                    for u in U:
                        act.wait_ge(LN["nf"]["tb"][u], v)
                        act.activation(tf["xn"][u], ps[:, bank[u][1], :], ACT.Identity,
                                       bias=WF[:, F_B:F_B + 1], scale=WF[:, F_G:F_G + 1]).then_inc(xn_r[u], 1)
                    for m in range(MF):
                        for u in U:
                            act.wait_ge(ag_mm[u], 2 * MF * (v - 1) + 2 * m + 1)
                            act.wait_ge(hf_r[u], MF * (v - 1) + m + 1)
                            act.activation(gf[u][0:FW[m], :], ps[0:FW[m], bank[u][(2 + 2 * m) % 4], :],
                                           ACT.Gelu, bias=WF[0:FW[m], F_BG + m:F_BG + m + 1])\
                                .then_inc(gate_r[u], 1)

        @block.vector
        def _(dve):
            dve.wait_ge(loaded, 64)

            def pre_norm(k):
                with dve.Fori(0, NB) as b:
                    v = k * NB + b + 1
                    for u in U:
                        kc = keep[:, ds(b * SEQ + COL * u, COL)]
                        if k == 0:
                            dve.tensor_copy(ta["z"][u], kc).then_inc(LN["pre"]["z"][u], 1)
                        else:
                            dve.wait_ge(kept[u], b + 1)
                            dve.tensor_tensor(ta["z"][u], kc, X[:, ds(seq_col(b, COL * u), COL)], ALU.add)\
                                .then_inc(LN["pre"]["z"][u], 1)
                    for u in U:
                        ln_stats(dve, "pre", u, v, bank[u][0], EPS_PRE)
                    for u in U:
                        ln_aggr(dve, "pre", u, v, EPS_PRE)
                    for u in U:
                        ln_norm(dve, "pre", u, v, bank[u][0], ta["zn"][u])

            pre_norm(0)
            with dve.Fori(0, BLOCKS) as l:
                dve.wait_ge(la1, 16 * (l + 1))
                dve.tensor_scalar(bias1[:, 0:2], Wa1[:, A1_B:A1_B + 2], 1.0, None, ALU.add).then_inc(biased, 1)
                hold(dve, biased, l + 1)
                with dve.Fori(0, NB) as b:
                    it = l * NB + b
                    for u in U:
                        dve.wait_ge(kvq[u], it + 1)
                        dve.tensor_scalar(ta["mk"][u], ps[:, bank[u][0], :], Wa1[:, A1_B:A1_B + 1], 0.0,
                                          ALU.add, ALU.min).then_inc(mins[u], 1)
                        dve.tensor_scalar(ta["den"][u], ps[:, bank[u][1], :], Wa1[:, A1_B + 1:A1_B + 2], 0.0,
                                          ALU.add, ALU.min).then_inc(mins[u], 1)
                    for u in U:
                        dve.wait_ge(exps[u], 2 * it + 1)
                        dve.scalar_tensor_tensor(ta["K"][u], ps[:, bank[u][0], :], bias1[:, 0:1], ta["ek"][u],
                                                 ALU.add, ALU.max, accum_out=kvp[:, u, 0:1])\
                            .then_inc(vprep[u], 1)
                        dve.wait_ge(exps[u], 2 * it + 2)
                        dve.tensor_scalar(ta["Vb"][u], ta["Vb"][u], 1.0, 1.0, ALU.subtract, ALU.add)\
                            .then_inc(rounded[u], 1)
                    for u in U:
                        dve.wait_ge(rounded[u], it + 1)
                        dve.scalar_tensor_tensor(Qf[:, ds(b * SEQ + COL * u, COL)], ps[:, bank[u][1], :],
                                                 bias1[:, 1:2], ta["Vb"][u], ALU.add, ALU.max)
                    for u in U:
                        dve.wait_ge(vprep[u], it + 1 + 2 * NB * l)
                        dve.scalar_tensor_tensor(ta["z"][u], ps[:, bank[u][2], :], Wa1[:, A1_B + 2:A1_B + 3],
                                                 ta["K"][u], ALU.add, ALU.mult, accum_out=kvp[:, u, 1:2])\
                            .then_inc(kq_used[u], 1)
                    for u in U:
                        dve.wait_ge(kq_used[u], it + 2)
                    dve.tensor_tensor(kvs[:, ds(b, 1), :], kvp[:, 0:1, :], kvp[:, 1:2, :], ALU.add)\
                        .then_inc(ksum, 1)
                hold(dve, ksum, NB * (l + 1))
                with dve.Fori(0, NB) as b:
                    v = l * NB + b + 1
                    base = NB * (l + 1) + 2 * (v - 1)
                    for u in U:
                        dve.tensor_scalar(ta["den"][u], Qf[:, ds(b * SEQ + COL * u, COL)], kvs[:, ds(b, 1), 0],
                                          EPS_Z, ALU.mult, ALU.add).then_inc(vprep[u], 1)
                    for u in U:
                        dve.wait_ge(vprep[u], base + 1)
                        dve.reciprocal(ta["K"][u], ta["den"][u]).then_inc(vprep[u], 1)
                    for u in U:
                        dve.wait_ge(vprep[u], base + 2)
                        dve.scalar_tensor_tensor(ta["Vb"][u], Qf[:, ds(b * SEQ + COL * u, COL)],
                                                 kvs[:, ds(b, 1), 1], ta["K"][u], ALU.mult, ALU.mult)\
                            .then_inc(vready[u], 1)
                    for u in U:
                        dve.wait_ge(ga[u], v)
                        dve.tensor_tensor(ta["z"][u], ta["g"][u], X[:, ds(seq_col(b, COL * u), COL)], ALU.add)\
                            .then_inc(LN["n1"]["z"][u], 1)
                    for u in U:
                        ln_stats(dve, "n1", u, v, bank[u][1], EPS_A)
                    for u in U:
                        ln_aggr(dve, "n1", u, v, EPS_A)
                    for u in U:
                        ln_norm(dve, "n1", u, v, bank[u][1], ta["zn"][u])
                    for u in U:
                        dve.wait_ge(g2[u], v)
                        dve.tensor_tensor(ta["z"][u], ta["g"][u], ta["x1"][u], ALU.add)\
                            .then_inc(LN["n2"]["z"][u], 1)
                    for u in U:
                        ln_stats(dve, "n2", u, v, bank[u][0], EPS_A)
                    for u in U:
                        ln_aggr(dve, "n2", u, v, EPS_A)
                    for u in U:
                        ln_norm(dve, "n2", u, v, bank[u][0], ta["zn"][u])
            for u in U:
                dve.wait_ge(x_done[u], NB * (BLOCKS + 1) + 1)
            pre_norm(1)

            dve.wait_ge(consts, 8)
            with dve.Fori(0, LAYERS) as l:
                for u in U:
                    dve.wait_ge(x_done[u], NB * (BLOCKS + 2 + l) + 1)
                dve.wait_ge(lb, 16 * (l + 1))
                for i in range(4):
                    s = WB[:, B_SC + i * DH:B_SC + (i + 1) * DH].unsqueeze(1).to_broadcast([P, TS, DH])
                    dve.tensor_tensor(tables[:, i, :, :], rotary[:, i, :, :], s, ALU.mult).then_inc(tab_r, 1)
                dve.wait_ge(tab_r, 4 * (l + 1))

                def xs(n, r):
                    g = l * NT + n
                    c = tile_col(n)
                    if not isinstance(n, int) or n >= RING:
                        dve.wait_ge(v_mm, 2 * (g - RING) + 3)
                    dve.tensor_copy(xs_[r][0:64, :], X[0:64, ds(c, P)]).then_inc(xs_r, 1)
                    dve.tensor_copy(xs_[r][64:P, :], X[64:P, ds(c - 1, P)]).then_inc(xs_r, 1)

                def rotate(n, c):
                    g = l * NT + n
                    hc = COL // DH
                    dve.wait_ge(sq_r, QKC * g + c + 1)
                    if c == 0:
                        dve.wait_ge(tr_mm, 4 * g + 1)
                    o = 2 * (c // 2)
                    src = ps[:, c % 2, :].rearrange("p (h d) -> p h d", d=DH)
                    a = t1[:, c * COL:(c + 1) * COL].rearrange("p (h d) -> p h d", d=DH)
                    bdst = t2[:, c * COL:(c + 1) * COL].rearrange("p (h d) -> p h d", d=DH)
                    cos = tables[:, o, ds(n % TS, 1), :].to_broadcast([P, hc, DH])
                    dve.tensor_tensor(a, src, cos, ALU.mult)
                    if c == 0:
                        dve.wait_ge(add_r, QKC * g + 1)
                    for i in range(2):
                        here, there = slice(32 * i, 32 * i + 32), slice(32 - 32 * i, 64 - 32 * i)
                        sin = tables[:, o + 1, ds(n % TS, 1), here].to_broadcast([P, hc, 32])
                        k = dve.tensor_tensor(bdst[:, :, here], src[:, :, there], sin, ALU.mult)
                    k.then_inc(rot_r, 1)

                def sumsq(n, c):
                    dve.tensor_reduce(ssq[:, 8 * c:8 * c + 8],
                                      sq[:, c * COL:(c + 1) * COL].rearrange("p (h d) -> p h d", d=DH),
                                      AX_X, ALU.add).then_inc(red_r, 1)

                def clamp(n):
                    g = l * NT + n
                    dve.wait_ge(red_r, QKC * (g + 1) + 1)
                    dve.tensor_scalar(ssc[:, :], ssq[:, :], NORM_MIN, None, ALU.max).then_inc(ssc_r, 1)

                def roots(n):
                    g = l * NT + n
                    k = (3 * NEWTON + 1) * g
                    dve.wait_ge(ssc_r, g + 1)
                    dve.tensor_scalar(rinv[:, :].bitcast(I32), ssc[:, :].bitcast(I32), -0.5, ROOT_BITS,
                                      ALU.mult, ALU.add).then_inc(newton, 1)
                    for i in range(NEWTON):
                        dve.wait_ge(newton, k + 3 * i + 1)
                        dve.scalar_tensor_tensor(nwt[:, 0, :], rinv[:, :], -0.5, rinv[:, :], ALU.mult,
                                                 ALU.mult).then_inc(newton, 1)
                        dve.wait_ge(newton, k + 3 * i + 2)
                        dve.tensor_tensor(nwt[:, 1, :], nwt[:, 0, :], ssc[:, :], ALU.mult).then_inc(newton, 1)
                        dve.wait_ge(newton, k + 3 * i + 3)
                        dve.scalar_tensor_tensor(rinv[:, :], nwt[:, 1, :], 1.5, rinv[:, :], ALU.add,
                                                 ALU.mult).then_inc(newton, 1)

                def unit(n):
                    g = l * NT + n
                    dve.wait_ge(newton, (3 * NEWTON + 1) * (g + 1))
                    dve.wait_ge(add_r, QKC * (g + 1) + 1)
                    t3 = t1.rearrange("p (h d) -> p h d", d=DH)
                    dve.tensor_tensor(t3, t3, rinv[:, :].unsqueeze(2).to_broadcast([P, 2 * HEADS, DH]),
                                      ALU.mult).then_inc(qk_r, 1)

                def masked(n):
                    g = l * NT + n
                    dve.wait_ge(s_mm, g + 2)
                    for a in range(2):
                        m = maskt[:, ds(n % TS, 1), :].to_broadcast([P, NP, 2 * WIN])
                        i = dve.tensor_tensor(sc.rearrange("p (a h k) -> p a h k", a=2, h=NP)[:, a],
                                              ps[:, 4 + a, :].rearrange("p (h k) -> p h k", h=NP), m, ALU.add)
                    i.then_inc(s_rd, 1)
                    dve.wait_ge(s_rd, g + 2)
                    dve.tensor_reduce(mx[:, :], sc.rearrange("p (h k) -> p h k", h=HEADS), AX_X, ALU.max)\
                        .then_inc(max_r, 1)

                def totals(n):
                    g = l * NT + n
                    dve.wait_ge(exp_r, g + 1)
                    dve.tensor_reduce(rs[:, :], pe_.rearrange("p (h k) -> p h k", h=HEADS), AX_X, ALU.add)\
                        .then_inc(sum_r, 1)
                    dve.wait_ge(sum_r, g + 1)
                    dve.reciprocal(rr[:, :], rs[:, :]).then_inc(rec_r, 1)

                def turn_probs(n):
                    g = l * NT + n
                    dve.wait_ge(p_r, g + 1)
                    dve.wait_ge(ptd_r, g + 1)
                    dve.transpose(pt, pe_).then_inc(pt_r, 1)

                def residual(n):
                    g = l * NT + n
                    c = tile_col(n)
                    dve.wait_ge(wo_r, g + 2)
                    dve.tensor_tensor(Y[:, ds(c, P)], ps[:, 6, 0:P], X[:, ds(c, P)], ALU.add).then_inc(y_r, 1)

                def step(n, r):
                    if live(n + 1):
                        xs(n + 1, (r + 1) % RING)
                    if live(n - 1):
                        masked(n - 1)
                    if live(n - 3):
                        residual(n - 3)
                    if live(n + 1):
                        for c in (0, 1):
                            rotate(n + 1, c)
                            sumsq(n + 1, c)
                    if live(n - 1):
                        totals(n - 1)
                    if live(n + 1):
                        for c in (2, 3):
                            rotate(n + 1, c)
                            sumsq(n + 1, c)
                        clamp(n + 1)
                    if live(n - 1):
                        turn_probs(n - 1)
                    if live(n + 1):
                        roots(n + 1)
                        unit(n + 1)

                walk(dve, step)

                dve.wait_ge(lf, 16 * (l + 1))
                hold(dve, y_r, NT * (l + 1) + 1)
                with dve.Fori(0, NB) as b:
                    v = l * NB + b + 1
                    for u in U:
                        dve.wait_ge(LN["nf"]["tr"][u], v)
                        dve.tensor_copy(tf["xs"][u][64:P, :], Y[64:P, ds(seq_col(b, COL * u) - 1, COL)])\
                            .then_inc(xhi[u], 1)
                    for u in U:
                        ln_stats(dve, "nf", u, v, bank[u][0], EPS_F)
                    for u in U:
                        ln_aggr(dve, "nf", u, v, EPS_F)
                    for u in U:
                        ln_norm(dve, "nf", u, v, bank[u][0], tf["zn"][u])
                    for m in range(MF):
                        for u in U:
                            dve.wait_ge(gate_r[u], MF * (v - 1) + m + 1)
                            dve.wait_ge(ag_mm[u], 2 * MF * (v - 1) + 2 * m + 2)
                            dve.scalar_tensor_tensor(hf[u][0:FW[m], m, :],
                                                     ps[0:FW[m], bank[u][(3 + 2 * m) % 4], :],
                                                     WF[0:FW[m], F_BA + m:F_BA + m + 1], gf[u][0:FW[m], :],
                                                     ALU.add, ALU.mult).then_inc(hf_r[u], 1)
                    for u in U:
                        col = ds(seq_col(b, COL * u), COL)
                        dve.wait_ge(o_mm[u], v)
                        dve.scalar_tensor_tensor(X[:, col], ps[:, bank[u][0], :], WF[:, F_B2:F_B2 + 1],
                                                 Y[:, col], ALU.add, ALU.add).then_inc(x_done[u], 1)
            for u in U:
                dve.wait_ge(x_done[u], NB * (BLOCKS + 2 + LAYERS) + 1)
            with dve.Fori(0, NB) as b:
                dve.tensor_tensor(keep[:, ds(b * SEQ, SEQ)], keep[:, ds(b * SEQ, SEQ)],
                                  X[:, ds(seq_col(b, 0), SEQ)], ALU.add).then_inc(finals, 1)


def constant_tables():
    f = np.float32
    half = np.arange(0, DH, 2, dtype=f)
    inv = (f(1.0) / f(10000.0) ** (half / f(DH))).astype(f)
    t = np.arange(SEQ, dtype=f)
    fr = t[:, None] * inv[None, :]
    fr = np.concatenate([fr, fr], -1).astype(np.float64)
    base = ((half + f(0.4 * DH)) / f(1.4 * DH)).astype(f)
    power = (t - SEQ // 2) / (WIN // 2)
    scale = base[None, :].astype(np.float64) ** power[:, None]
    scale = np.concatenate([scale, scale], -1)
    sign = np.concatenate([-np.ones(DH // 2), np.ones(DH // 2)])
    cos, sin = np.cos(fr), np.sin(fr) * sign
    rot = np.stack([QK_SCALE * cos * scale, QK_SCALE * sin * scale, cos / scale, sin / scale]).astype(f)
    rot = rot.reshape(4, TS, P, DH).transpose(2, 0, 1, 3).reshape(P, 4 * TS * DH)
    i, j = np.arange(WIN)[:, None], np.arange(WIN)[None, :]
    before, own = np.where(i > j, NEG, 0.0), np.where(i < j, NEG, 0.0)
    mask = np.tile(np.concatenate([before, own], 1)[None, None], (TS, P // WIN, 1, 1))
    mask[0, 0, :, :WIN] = NEG
    mask = mask.reshape(TS, P, 2 * WIN).transpose(1, 0, 2).reshape(P, TS * 2 * WIN).astype(f)
    mask = np.concatenate([mask, np.tile((np.arange(TS) > 0).astype(f), (P, 1))], 1)
    return np.ascontiguousarray(rot), np.ascontiguousarray(mask)


def kernel(**inputs):
    import concourse.bacc as _bacc
    from concourse.bass_utils import run_bass_kernel_spmd as _run

    i = {k: np.asarray(v) for k, v in inputs.items()}
    A = {k[len("L0_attn_"):]: v for k, v in i.items() if k.startswith("L0_attn_")}
    B = {k[len("L0_ffn_"):]: v for k, v in i.items() if k.startswith("L0_ffn_")}

    def col(v):
        return v[:, :, None]

    def chunks(w, n, rows):
        full = np.zeros((w.shape[0], n * P, w.shape[2]), w.dtype)
        full[:, :rows] = w
        return full.reshape(w.shape[0], n, P, -1).transpose(0, 2, 1, 3).reshape(w.shape[0], P, -1)

    wa1 = np.concatenate([A["Wq"], A["Wk"], A["Wv"], col(A["bk"]), col(A["bq"]), col(A["bv"])], 2)
    wa2 = np.concatenate([A["Wo"], A["Wf1"], chunks(A["Wf2"], MA, FA), col(A["bo"]), col(A["ln1_s"]),
                          col(A["ln1_b"]), chunks(col(A["bf1"]), MA, FA), col(A["bf2"]), col(A["ln2_s"]),
                          col(A["ln2_b"])], 2)

    def spread(v):
        return np.broadcast_to(v[:, None, :], (LAYERS, P, DH))

    def swap(v):
        return np.concatenate([v[:, DH // 2:], v[:, :DH // 2]], 1)

    qs, ks = B["q_scale"], B["k_scale"]
    wb = np.concatenate([B["Wqkv"], chunks(B["Wo"], NP, INNER), spread(qs), spread(swap(qs)), spread(ks),
                         spread(swap(ks))], 2)
    wf = np.concatenate([B["W1"], chunks(B["W2"], MF, HID), col(B["ln_g"]), col(B["ln_b"]),
                         chunks(col(B["b1"][:, :HID]), MF, HID), chunks(col(B["b1"][:, HID:]), MF, HID),
                         col(B["b2"])], 2)
    rot, mask = constant_tables()
    arrays = {"xT": A["x"].reshape(NB * SEQ, D).T, "wa1": wa1.reshape(-1, A1_W), "wa2": wa2.reshape(-1, A2_W),
              "wb": wb.reshape(-1, B_W), "wf": wf.reshape(-1, F_W), "rot": rot, "mask": mask}
    arrays = {k: np.ascontiguousarray(v) for k, v in arrays.items()}
    nc = _bacc.Bacc("TRN2", target_bir_lowering=False, num_devices=1)
    args = [nc.dram_tensor(k, v.shape, F32, kind="ExternalInput").ap() for k, v in arrays.items()]
    out = nc.dram_tensor("outT", [D, NB * SEQ], F32, kind="ExternalOutput").ap()
    build(nc, *args, out)
    r = _run(nc, [arrays], core_ids=[0])
    return np.ascontiguousarray(r.results[0]["outT"].T).reshape(NB, SEQ, D)
```

```python
from contextlib import ExitStack

import numpy as np
import concourse.bass as bass
from concourse import mybir

F32 = mybir.dt.float32
I32 = mybir.dt.int32
ALU = mybir.AluOpType
ACT = mybir.ActivationFunctionType
AX_X = mybir.AxisListType.X
ds = bass.ds

P = 128
NB, SEQ, D = 4, 1024, 128
BLOCKS, FA = 8, 512
MA = FA // P
LAYERS, HEADS, DH, WIN = 6, 16, 64, 32
INNER = HEADS * DH
HID = int(D * 4 * 2 / 3)
MF = -(-HID // P)
FW = [min(P, HID - P * m) for m in range(MF)]
COL = 512
UT = SEQ // COL
NC = NB * UT
TS = SEQ // P
NT = NB * TS
SP1 = SEQ + 1
NP = HEADS // 2
QKC = 2 * INNER // COL
RING = 3
HEAD, TAIL = range(-2, 3), range(NT - 2, NT + 3)
NEG = -1.0e30
EPS_PRE, EPS_A, EPS_F, EPS_Z = 1e-5, 1e-6, 1e-5, 1e-6
NORM_MIN = 1e-24
QK_SCALE = 8.0
ROOT_BITS = 1597463007.0
NEWTON = 3

A1_B = 3 * D
A1_W = A1_B + 3
A2_F1, A2_F2 = D, D + FA
A2_V = A2_F2 + MA * D
A2_BO, A2_S1, A2_B1, A2_BF1 = A2_V, A2_V + 1, A2_V + 2, A2_V + 3
A2_BF2 = A2_BF1 + MA
A2_S2, A2_B2 = A2_BF2 + 1, A2_BF2 + 2
A2_W = A2_B2 + 1
B_WO = 3 * INNER
B_SC = B_WO + NP * D
B_W = B_SC + 4 * DH
F_W2 = 2 * HID
F_G = F_W2 + MF * D
F_B = F_G + 1
F_BA = F_B + 1
F_BG = F_BA + MF
F_B2 = F_BG + MF
F_W = F_B2 + 1


def build(nc, xT, wa1, wa2, wb, wf, rot, mask, outT):
    with ExitStack() as ctx:
        def sb(name, shape):
            return ctx.enter_context(nc.sbuf_tensor(name, shape, F32))

        def sem(name):
            return ctx.enter_context(nc.semaphore(name))

        def pair(name):
            return [sem(f"{name}_{u}") for u in range(UT)]

        ps = ctx.enter_context(nc.psum_tensor("ps", [P, 8, COL], F32))

        X = sb("X", [P, NB * SP1])
        Y = sb("Y", [P, NB * SP1])
        keep = sb("keep", [P, NB * SEQ])
        ident = sb("ident", [P, P])
        power = sb("power", [P, 4])
        WB = sb("WB", [P, B_W])
        WF = sb("WF", [P, F_W])
        rotary = sb("rotary", [P, 4, TS, DH])
        tables = sb("tables", [P, 4, TS, DH])
        maskt = sb("maskt", [P, TS, 2 * WIN])
        inside = sb("inside", [P, TS])
        stats = sb("stats", [P, UT, 4, 6])
        mv = sb("mv", [P, UT, 4, 2])
        ve = sb("ve", [P, UT, 4])
        rstd = sb("rstd", [P, UT, 4])
        mneg, shift = sb("mneg", [P, 4]), sb("shift", [P, 4])
        kvp = sb("kvp", [P, UT, 2])
        kvs = sb("kvs", [P, NB, 2])
        bias1 = sb("bias1", [P, 3])
        ssq = sb("ssq", [P, 2 * HEADS])
        ssc = sb("ssc", [P, 2 * HEADS])
        nwt = sb("nwt", [P, 2, 2 * HEADS])
        rinv = sb("rinv", [P, 2 * HEADS])
        mx = sb("mx", [P, HEADS])
        rs = sb("rs", [P, HEADS])
        rr = sb("rr", [P, HEADS])

        arena = sb("arena", [P, 24600])

        def carve(sizes):
            at, got = 0, []
            for n in sizes:
                got.append(arena[:, at:at + n])
                at += n
            return got

        (Wa1, Wa2, Qf, *rest) = carve([A1_W, A2_W, NB * SEQ] + [COL] * (UT * 13))
        ta = {k: [rest[i * UT + u] for u in range(UT)]
              for i, k in enumerate(["mk", "ek", "K", "den", "Vb", "g", "z", "zn", "x1"])}
        ha = [arena[:, A1_W + A2_W + NB * SEQ + COL * (18 + MA * u):][:, 0:MA * COL]
              .rearrange("p (m n) -> p m n", m=MA) for u in range(UT)]
        den, recip, Vb, x1, h_ = ta["den"][0], ta["K"][0], ta["Vb"][0], ta["x1"], ha[0]
        (g1, g2), (z1, z2), (zn1, zn2) = ta["g"], ta["z"], ta["zn"]
        WO_BANK, TURN_BANK, BACK_BANK, F1_BANK, F2_BANK = 0, (1, 3), (2, 4), 5, 7
        (t1, t2, sq, sc, pe_, pt, PTd, qTf, kTf, OTf, *rings) = carve(
            [2 * INNER] * 3 + [INNER] * 3 + [2 * HEADS * P] + [INNER] + [NP * (WIN + P)] + [INNER]
            + [INNER] * (2 * RING) + [P] * RING)
        v_, vs_, xs_ = rings[:RING], rings[RING:2 * RING], rings[2 * RING:]
        qT = qTf.rearrange("p (c t) -> p c t", c=NP)
        kT = kTf.rearrange("p (c t) -> p c t", c=NP)
        OT = OTf.rearrange("p (c t) -> p c t", c=NP)
        fa = arena[:, 0:7 * INNER].rearrange("p (k n) -> p k n", n=COL)
        tf = {k: [fa[:, i * UT + u, :] for u in range(UT)] for i, k in enumerate(["xs", "zn", "xn"])}
        gf = [fa[:, 6 + u, :] for u in range(UT)]
        hf = [fa[:, 8 + MF * u:8 + MF * u + MF, :] for u in range(UT)]

        loaded, consts = sem("loaded"), sem("consts")
        la1, la2, lb, lf = sem("wa1_in"), sem("wa2_in"), sem("wb_in"), sem("wf_in")
        stored = sem("stored")
        x_done = pair("x_done")

        LN = {k: {s: pair(f"{k}_{s}") for s in ("z", "tr", "stat", "rstd", "zn", "tb")}
              for k in ("pre", "n1", "n2", "nf")}
        xlo, xhi = pair("xs_lo"), LN["nf"]["z"]
        kept = pair("kept")
        kvq, mins, exps, kq_used = pair("kvq_mm"), pair("mins"), pair("exps"), pair("kvq_used")
        rounded = pair("q_rounded")
        ksum = sem("seq_sums")
        biased = sem("bias1_ready")
        k_sum = pair("k_sum")
        mneg_r, shifts = sem("n2_mean_ready"), sem("n2_shift_ready")
        vprep, vready, wo_mm, ga = sem("v_chain"), sem("v_ready"), sem("wo_mm"), sem("attn_gelu")
        x1_r, f1_mm, h_r, f2_mm, g2_r = map(sem, ("x1_ready", "f1_mm", "h_ready", "f2_mm", "ff_gelu"))

        xn_r, ag_mm, gate_r, hf_r, o_mm = map(pair, ("xn_r", "ag_mm", "gate_r", "hf_r", "o_mm"))
        finals, passed = sem("finals"), sem("waits_passed")

        (tab_r, xs_r, qk_mm, v_mm, sq_r, rot_r, add_r, red_r, ssc_r, newton, q_r, k_r, tr_mm, shift_r, tr_ev,
         s_mm, s_rd, max_r, sub_r, exp_r, sum_r, rec_r, p_r, pt_r, ptd_r, pv_mm, ot_r, wo_r, y_r, v_r,
         vs_in) = map(sem, (
             "tables_ready", "xs_ready", "qk_mm", "v_mm", "squares", "rotated", "added", "sumsq",
             "sumsq_clamped", "newton", "q_ready", "k_ready", "transposed", "keys_shifted", "transposes_out",
             "scores_mm", "scores_masked", "max_ready", "shifted", "exp_ready", "sum_ready", "recip_ready",
             "probs_ready", "probsT_ready", "probsT_wide", "pv_mm", "ot_ready", "wo_done", "y_ready",
             "v_ready_b", "vshift_in"))

        def seq_col(b, t):
            return b * SP1 + 1 + t

        def tile_col(n):
            return n * P + n // TS + 1

        def hold(eng, s, v):
            eng.wait_ge(s, v)
            eng.sem_inc(passed, 1)

        def live(n):
            return not isinstance(n, int) or 0 <= n < NT

        def walk(eng, step):
            for n in HEAD:
                step(n, n % RING)
            with eng.Fori(0, (TAIL[0] - HEAD[-1] - 1) // RING) as j:
                for i in range(RING):
                    step(RING * j + HEAD[-1] + 1 + i, (HEAD[-1] + 1 + i) % RING)
            for n in TAIL:
                step(n, n % RING)

        def at(tile):
            return tile[0] + tile[1] // UT, tile[1] % UT

        def has(tile):
            return not isinstance(tile[0], int) or 0 <= UT * tile[0] + tile[1] < NC

        def by(tile, d):
            return tile[0], tile[1] + d

        def upto(l, tile):
            return l * NC + UT * tile[0] + tile[1] + 1

        def x_col(tile):
            b, u = at(tile)
            return ds(seq_col(b, COL * u), COL)

        def q_col(tile):
            b, u = at(tile)
            return ds(b * SEQ + COL * u, COL)

        def march(eng, step):
            for k in range(-3, 1):
                step((0, k))
            with eng.Fori(0, (NC - 4) // UT) as j:
                step((j, 1))
                step((j, 2))
            for k in range(NC - 3, NC + 1):
                step((0, k))

        def heads(ap):
            return ap.rearrange("p (h d) -> p h d", d=DH)

        def c4(ap):
            return ap.rearrange("p (j t) -> p j t", j=4)

        def ln_turn(pe, k, u, v, src, bank):
            pe.wait_ge(LN[k]["z"][u], v)
            for j in range(4):
                i = pe.transpose(ps[:, bank, j * P:(j + 1) * P], src[:, j * P:(j + 1) * P], ident[:, :])
            i.then_inc(LN[k]["tr"][u], 1)

        def ln_stats(dve, k, u, v, bank, eps):
            st = LN[k]["stat"][u]
            dve.wait_ge(LN[k]["tr"][u], v + 1)
            for j in range(4):
                i = dve.bn_stats(stats[:, u, j, :], ps[:, bank, j * P:(j + 1) * P])
            i.then_inc(st, 1)

        def ln_aggr(dve, k, u, v, eps):
            st = LN[k]["stat"][u]
            hold(dve, st, 3 * v - 2)
            for j in range(4):
                i = dve.bn_aggr(mv[:, u, j, :], stats[:, u, j, :])
            i.then_inc(st, 1)
            dve.wait_ge(st, 3 * v - 1)
            dve.tensor_scalar(ve[:, u, :], mv[:, u, :, 1], eps, None, ALU.add).then_inc(st, 1)

        def ln_rstd(pool, k, u, v):
            pool.wait_ge(LN[k]["stat"][u], 3 * v)
            pool.tensor_tensor(rstd[:, u, :], ve[:, u, :], power[:, 0:4], ALU.pow)\
                .then_inc(LN[k]["rstd"][u], 1)

        def ln_norm(dve, k, u, v, bank, dst):
            dve.wait_ge(LN[k]["rstd"][u], v)
            for j in range(4):
                i = dve.tensor_scalar(dst[:, j * P:(j + 1) * P], ps[:, bank, j * P:(j + 1) * P],
                                      mv[:, u, j, 0:1], rstd[:, u, j:j + 1], ALU.subtract, ALU.mult)
            i.then_inc(LN[k]["zn"][u], 1)

        def ln_back(pe, k, u, v, src, bank):
            pe.wait_ge(LN[k]["zn"][u], v)
            for j in range(4):
                i = pe.transpose(ps[:, bank, j * P:(j + 1) * P], src[:, j * P:(j + 1) * P], ident[:, :])
            i.then_inc(LN[k]["tb"][u], 1)

        U = range(UT)
        bank = [[4 * u + i for i in range(4)] for u in U]
        block = ctx.enter_context(nc.Block())

        @block.sync
        def _(sp):
            for s in (v_mm, tr_mm, wo_r, v_r, s_rd, y_r, ptd_r, red_r, s_mm, pt_r, pv_mm, vs_in, add_r,
                      *kq_used, *hf_r, *kept, *x_done, *(q for k in LN.values() for q in k["tr"])):
                sp.sem_inc(s, 1)
            sp.dma_start(keep[:, :], xT).then_inc(loaded, 16)
            sp.dma_start(rotary[:, :, :, :].rearrange("p a b c -> p (a b c)"), rot).then_inc(loaded, 16)
            sp.dma_start(maskt[:, :, :].rearrange("p a b -> p (a b)"), mask[:, 0:TS * 2 * WIN]).then_inc(loaded, 16)
            sp.dma_start(inside[:, :], mask[:, TS * 2 * WIN:]).then_inc(loaded, 16)
            with sp.Fori(0, BLOCKS) as l:
                for u in U:
                    hold(sp, kq_used[u], NB * l + 1)
                sp.dma_start(Wa1, wa1[ds(l * P, P), :]).then_inc(la1, 16)
                for u in U:
                    hold(sp, x_done[u], NB * (l + 1) + 1)
                sp.dma_start(Wa2, wa2[ds(l * P, P), :]).then_inc(la2, 16)
            with sp.Fori(0, LAYERS) as l:
                hold(sp, v_mm, NT * 2 * l + 1)
                hold(sp, wo_r, NT * l + 1)
                sp.dma_start(WB[:, :], wb[ds(l * P, P), :]).then_inc(lb, 16)
                for u in U:
                    hold(sp, x_done[u], NB * (BLOCKS + 2 + l) + 1)
                sp.dma_start(WF[:, :], wf[ds(l * P, P), :]).then_inc(lf, 16)

                def vshift(n, r):
                    if not live(n):
                        return
                    g = l * NT + n
                    hold(sp, v_r, 2 * g + 3)
                    sp.dma_start(vs_[r][WIN:P, :], v_[r][0:P - WIN, :]).then_inc(vs_in, 16)
                    sp.dma_start(vs_[r][0:WIN, :], v_[r - 1][P - WIN:P, :]).then_inc(vs_in, 16)

                walk(sp, vshift)
            sp.wait_ge(finals, NB)
            sp.dma_start(outT, keep[:, :]).then_inc(stored, 16)
            sp.wait_ge(stored, 16)

        @block.gpsimd
        def _(pool):
            pool.memset(ident[:, :], 0.0).then_inc(consts, 1)
            pool.memset(power[:, :], -0.5).then_inc(consts, 1)
            pool.wait_ge(consts, 1)
            pool.affine_select(out=ident[:, :], in_=ident[:, :], compare_op=ALU.not_equal, fill=1.0, base=0,
                               pattern=[[-1, P]], channel_multiplier=1).then_inc(consts, 1)
            pool.memset(X[:, :], 0.0).then_inc(consts, 1)
            pool.memset(Y[:, :], 0.0).then_inc(consts, 1)
            pool.wait_ge(consts, 5)

            def pre_norm(k):
                with pool.Fori(0, NB) as b:
                    for u in U:
                        ln_rstd(pool, "pre", u, k * NB + b + 1)

            pre_norm(0)
            with pool.Fori(0, BLOCKS) as l:
                def step(t):
                    if has(by(t, 1)):
                        ln_rstd(pool, "n1", 0, upto(l, by(t, 1)))
                    if has(by(t, -1)):
                        w = upto(l, by(t, -1))
                        ln_rstd(pool, "n2", 1, w)
                        pool.wait_ge(mneg_r, w)
                        pool.wait_ge(LN["n2"]["rstd"][1], w)
                        pool.tensor_tensor(shift[:, :], mneg[:, :], rstd[:, 1, :], ALU.mult)\
                            .then_inc(shifts, 1)

                march(pool, step)
            pre_norm(1)
            for u in U:
                pool.wait_ge(x_done[u], NB * (BLOCKS + 2) + 1)
            pool.memset(PTd, 0.0).then_inc(consts, 1)
            pool.memset(kTf, 0.0).then_inc(consts, 1)
            pool.memset(v_[RING - 1], 0.0).then_inc(consts, 1)
            with pool.Fori(0, LAYERS) as l:
                def probs_sub(n):
                    g = l * NT + n
                    pool.wait_ge(max_r, g + 1)
                    s3 = sc.rearrange("p (h k) -> p h k", h=HEADS)
                    pool.tensor_tensor(s3, s3, mx[:, :].unsqueeze(2).to_broadcast([P, HEADS, 2 * WIN]),
                                       ALU.subtract).then_inc(sub_r, 1)

                def probs_norm(n):
                    g = l * NT + n
                    pool.wait_ge(rec_r, g + 1)
                    p3 = pe_.rearrange("p (h k) -> p h k", h=HEADS)
                    pool.tensor_tensor(p3, p3, rr[:, :].unsqueeze(2).to_broadcast([P, HEADS, 2 * WIN]),
                                       ALU.mult).then_inc(p_r, 1)

                def add(n, c):
                    g = l * NT + n
                    pool.wait_ge(rot_r, QKC * g + c + 1)
                    w = slice(c * COL, (c + 1) * COL)
                    pool.tensor_tensor(t1[:, w], t1[:, w], t2[:, w], ALU.add).then_inc(add_r, 1)

                def unit(n):
                    g = l * NT + n
                    pool.wait_ge(newton, (3 * NEWTON + 1) * (g + 1))
                    pool.wait_ge(add_r, QKC * (g + 1) + 1)
                    t3 = heads(t1)[:, HEADS:2 * HEADS, :]
                    pool.tensor_tensor(t3, t3, rinv[:, HEADS:2 * HEADS].unsqueeze(2).to_broadcast([P, HEADS, DH]),
                                       ALU.mult).then_inc(k_r, 1)

                def step(n, r):
                    if live(n - 1):
                        probs_sub(n - 1)
                    if live(n + 1):
                        add(n + 1, 0)
                        add(n + 1, 1)
                    if live(n - 1):
                        probs_norm(n - 1)
                    if live(n + 1):
                        add(n + 1, 2)
                        add(n + 1, 3)
                        unit(n + 1)

                walk(pool, step)
                with pool.Fori(0, NB) as b:
                    for u in U:
                        ln_rstd(pool, "nf", u, l * NB + b + 1)

        @block.tensor
        def _(pe):
            pe.wait_ge(consts, 3)

            def pre_norm(k):
                with pe.Fori(0, NB) as b:
                    v = k * NB + b + 1
                    for u in U:
                        ln_turn(pe, "pre", u, v, ta["z"][u], bank[u][0])
                    for u in U:
                        pe.wait_ge(x_done[u], k * NB * (BLOCKS + 1) + b + 1)
                        ln_back(pe, "pre", u, v, ta["zn"][u], bank[u][1])

            pre_norm(0)
            with pe.Fori(0, BLOCKS) as l:
                pe.wait_ge(la1, 16 * (l + 1))
                for u in U:
                    hold(pe, x_done[u], NB * (l + 1) + 1)
                with pe.Fori(0, NB) as b:
                    it = l * NB + b
                    for u in U:
                        pe.wait_ge(kq_used[u], it + 1)
                        xcol = X[:, ds(seq_col(b, COL * u), COL)]
                        for i, w in enumerate((1, 0, 2)):
                            m = pe.matmul(ps[:, bank[u][i], :], Wa1[:, w * D:(w + 1) * D], xcol,
                                          start=True, stop=True)
                        m.then_inc(kvq[u], 1)
                hold(pe, la2, 16 * (l + 1))
                def project(t):
                    v = upto(l, t)
                    pe.wait_ge(vready, v)
                    pe.matmul(ps[:, WO_BANK, :], Wa2[:, 0:D], Vb, start=True, stop=True).then_inc(wo_mm, 1)

                def hidden(t):
                    v = upto(l, t)
                    pe.wait_ge(x1_r, v)
                    for m in range(MA):
                        if m >= 2:
                            pe.wait_ge(h_r, MA * (v - 1) + m - 1)
                        pe.matmul(ps[:, F1_BANK + m % 2, :], Wa2[:, A2_F1 + m * P:A2_F1 + (m + 1) * P],
                                  x1[at(t)[1]], start=True, stop=True).then_inc(f1_mm, 1)

                def down(t):
                    v = upto(l, t)
                    for m in range(MA):
                        pe.wait_ge(h_r, MA * (v - 1) + m + 1)
                        i = pe.matmul(ps[:, F2_BANK, :], Wa2[:, A2_F2 + m * D:A2_F2 + (m + 1) * D],
                                      h_[:, m, :], start=(m == 0), stop=(m == MA - 1))
                    i.then_inc(f2_mm, 1)

                def step(t):
                    if has(t):
                        hidden(t)
                    if has(by(t, -1)):
                        ln_turn(pe, "n2", 1, upto(l, by(t, -1)), z2, TURN_BANK[1])
                    if has(by(t, 1)):
                        ln_back(pe, "n1", 0, upto(l, by(t, 1)), zn1, BACK_BANK[0])
                    if has(by(t, 2)):
                        project(by(t, 2))
                    if has(t):
                        down(t)
                    if has(by(t, -1)):
                        b, u = at(by(t, -2))
                        pe.wait_ge(x_done[u], NB * (l + 1) + b + 2)
                        ln_back(pe, "n2", 1, upto(l, by(t, -1)), zn2, BACK_BANK[1])
                    if has(by(t, 2)):
                        ln_turn(pe, "n1", 0, upto(l, by(t, 2)), z1, TURN_BANK[0])

                march(pe, step)
            pre_norm(1)

            pe.wait_ge(consts, 8)
            with pe.Fori(0, LAYERS) as l:
                def project(n, r, c):
                    g = l * NT + n
                    if c == 0:
                        pe.wait_ge(xs_r, 2 * g + 2)
                    if c < 2:
                        pe.wait_ge(v_r, 2 * g + 1)
                    else:
                        pe.wait_ge(rot_r, QKC * g + c - 1)
                    pe.matmul(ps[:, c % 2, :], xs_[r], WB[:, c * COL:(c + 1) * COL], start=True,
                              stop=True).then_inc(qk_mm if c < QKC else v_mm, 1)

                def turn(n):
                    g = l * NT + n
                    for r in range(4):
                        if r % 2 == 0:
                            pe.wait_ge(q_r if r == 0 else k_r, g + 1)
                        if r >= 2:
                            pe.wait_ge(tr_ev, 4 * g + r - 1)
                        for j in range(4):
                            c = 4 * r + j
                            i = pe.transpose(ps[:, 2 + r % 2, j * P:(j + 1) * P],
                                             t1[:, c * P:(c + 1) * P], ident[:, :])
                        i.then_inc(tr_mm, 1)

                def scores(n, windows):
                    g = l * NT + n
                    if windows[0] == 0:
                        pe.wait_ge(s_rd, g + 1)
                        hold(pe, tr_ev, 4 * g + 4)
                    for w in windows:
                        for h in range(HEADS):
                            r = 64 * (h % 2)
                            i = pe.matmul(ps[WIN * w:WIN * (w + 1), 4 + h % 2, (h // 2) * 64:(h // 2) * 64 + 64],
                                          qT[r:r + 64, h // 2, WIN * w:WIN * (w + 1)],
                                          kT[r:r + 64, h // 2, WIN * w:WIN * (w + 2)], start=True, stop=True)
                    if w == 3:
                        i.then_inc(s_mm, 1)

                def attend(n, r, half):
                    g = l * NT + n
                    if half == 0:
                        pe.wait_ge(ptd_r, g + 2)
                        pe.wait_ge(vs_in, 32 * (g + 1) + 1)
                        pe.wait_ge(y_r, g + 1)
                    pw = PTd.rearrange("p (a c k q) -> p a c k q", a=2, c=NP, k=2)
                    for c in range(4 * half, 4 * half + 4):
                        for part, val in ((1, v_[r]), (0, vs_[r])):
                            for a in range(2):
                                h = 2 * c + a
                                i = pe.matmul(ps[64 * a:64 * a + 64, 6 + half, (c % 4) * P:(c % 4 + 1) * P],
                                              val[:, h * DH:(h + 1) * DH], pw[:, a, c, part, :],
                                              start=(part == 1), stop=(part == 0))
                    i.then_inc(pv_mm, 1)

                def output(n):
                    g = l * NT + n
                    for c in range(NP):
                        if c % 4 == 0:
                            pe.wait_ge(ot_r, 2 * g + 1 + c // 4)
                        i = pe.matmul(ps[:, 6, 0:P], WB[:, B_WO + c * D:B_WO + (c + 1) * D], OT[:, c, :],
                                      start=(c == 0), stop=(c == NP - 1))
                    i.then_inc(wo_r, 1)

                def step(n, r):
                    new, old = (r + 1) % RING, (r - 2) % RING
                    if live(n):
                        turn(n)
                    if live(n - 2):
                        attend(n - 2, old, 0)
                    if live(n + 1):
                        project(n + 1, new, 2)
                    if live(n - 2):
                        attend(n - 2, old, 1)
                    if live(n + 1):
                        project(n + 1, new, 3)
                    if live(n):
                        scores(n, (0,))
                    if live(n + 1):
                        project(n + 1, new, 4)
                    if live(n):
                        scores(n, (1,))
                    if live(n + 1):
                        project(n + 1, new, 5)
                    if live(n):
                        scores(n, (2, 3))
                    if live(n - 2):
                        output(n - 2)
                    if live(n + 2):
                        project(n + 2, (r + 2) % RING, 0)
                        project(n + 2, (r + 2) % RING, 1)

                pe.wait_ge(lb, 16 * (l + 1))
                walk(pe, step)

                hold(pe, lf, 16 * (l + 1))
                with pe.Fori(0, NB) as b:
                    v = l * NB + b + 1
                    for u in U:
                        pe.wait_ge(xlo[u], v)
                        ln_turn(pe, "nf", u, v, tf["xs"][u], bank[u][0])
                    for u in U:
                        ln_back(pe, "nf", u, v, tf["zn"][u], bank[u][1])
                    for m in range(MF):
                        for u in U:
                            if m == 0:
                                pe.wait_ge(xn_r[u], v)
                            if m == 2:
                                pe.wait_ge(hf_r[u], MF * (v - 1) + 2)
                            for k in (1, 0):
                                pe.matmul(ps[0:FW[m], bank[u][(2 + 2 * m + 1 - k) % 4], :],
                                          WF[:, k * HID + m * P:k * HID + m * P + FW[m]], tf["xn"][u],
                                          start=True, stop=True).then_inc(ag_mm[u], 1)
                    for u in U:
                        for m in range(MF):
                            if m == 0:
                                pe.wait_ge(hf_r[u], MF * (v - 1) + 2 + 1)
                            elif m == 2:
                                pe.wait_ge(hf_r[u], MF * v + 1)
                            i = pe.matmul(ps[:, bank[u][0], :], WF[0:FW[m], F_W2 + m * D:F_W2 + (m + 1) * D],
                                          hf[u][0:FW[m], m, :], start=(m == 0), stop=(m == MF - 1))
                        i.then_inc(o_mm[u], 1)

        @block.scalar
        def _(act):
            def pre_norm(k):
                with act.Fori(0, NB) as b:
                    v = k * NB + b + 1
                    for u in U:
                        if k:
                            act.wait_ge(LN["pre"]["z"][u], v)
                            act.activation(keep[:, ds(b * SEQ + COL * u, COL)], ta["z"][u], ACT.Copy)\
                                .then_inc(kept[u], 1)
                    for u in U:
                        act.wait_ge(LN["pre"]["tb"][u], v)
                        act.activation(X[:, ds(seq_col(b, COL * u), COL)], ps[:, bank[u][1], :], ACT.Copy)\
                            .then_inc(x_done[u], 1)

            act.wait_ge(consts, 5)
            pre_norm(0)
            with act.Fori(0, BLOCKS) as l:
                with act.Fori(0, NB) as b:
                    v = l * NB + b + 1
                    for u in U:
                        for i, k in enumerate(("ek", "K")):
                            act.wait_ge(mins[u], 2 * v - 1 + i)
                            src = ta["mk"][u] if i == 0 else ta["den"][u]
                            act.activation(ta["ek"][u] if i == 0 else ta["Vb"][u], src, ACT.Exp)\
                                .then_inc(exps[u], 1)
                hold(act, la2, 16 * (l + 1))
                def vec(c):
                    return Wa2[:, c:c + 1]

                def attn_gelu(t):
                    act.wait_ge(wo_mm, upto(l, t))
                    act.activation(g1, ps[:, WO_BANK, :], ACT.Gelu_apprx_tanh, bias=vec(A2_BO)).then_inc(ga, 1)

                def first_norm(t):
                    act.wait_ge(LN["n1"]["tb"][0], upto(l, t))
                    act.activation(x1[at(t)[1]], ps[:, BACK_BANK[0], :], ACT.Identity, bias=vec(A2_B1),
                                   scale=vec(A2_S1)).then_inc(x1_r, 1)

                def hidden(t):
                    for m in range(MA):
                        act.wait_ge(f1_mm, MA * (upto(l, t) - 1) + m + 1)
                        act.activation(h_[:, m, :], ps[:, F1_BANK + m % 2, :], ACT.Gelu_apprx_tanh,
                                       bias=vec(A2_BF1 + m)).then_inc(h_r, 1)

                def ff_gelu(t):
                    act.wait_ge(f2_mm, upto(l, t))
                    act.activation(g2, ps[:, F2_BANK, :], ACT.Gelu_apprx_tanh, bias=vec(A2_BF2))\
                        .then_inc(g2_r, 1)

                def second_unit(t):
                    act.wait_ge(shifts, upto(l, t))
                    for j in range(4):
                        i = act.activation(zn2[:, j * P:(j + 1) * P], ps[:, TURN_BANK[1], j * P:(j + 1) * P],
                                           ACT.Identity, bias=shift[:, j:j + 1], scale=rstd[:, 1, j:j + 1])
                    i.then_inc(LN["n2"]["zn"][1], 1)

                def second_norm(t):
                    act.wait_ge(LN["n2"]["tb"][1], upto(l, t))
                    act.activation(X[:, x_col(t)], ps[:, BACK_BANK[1], :], ACT.Identity, bias=vec(A2_B2),
                                   scale=vec(A2_S2)).then_inc(x_done[at(t)[1]], 1)

                def step(t):
                    if has(t):
                        hidden(t)
                    if has(by(t, 1)):
                        first_norm(by(t, 1))
                    if has(by(t, 2)):
                        attn_gelu(by(t, 2))
                    if has(by(t, -1)):
                        second_unit(by(t, -1))
                    if has(t):
                        ff_gelu(t)
                    if has(by(t, -1)):
                        second_norm(by(t, -1))

                march(act, step)
            pre_norm(1)

            act.wait_ge(consts, 8)
            act.wait_ge(loaded, 64)
            with act.Fori(0, LAYERS) as l:
                def square(n, c):
                    g = l * NT + n
                    act.wait_ge(qk_mm, QKC * g + c + 1)
                    if c == 0:
                        act.wait_ge(red_r, QKC * g + 1)
                    act.activation(sq[:, c * COL:(c + 1) * COL], ps[:, c % 2, :], ACT.Square)\
                        .then_inc(sq_r, 1)

                def keys_on(n):
                    g = l * NT + n
                    act.wait_ge(s_mm, g + 1)
                    act.activation(kT[:, :, 0:WIN], kT[:, :, P:P + WIN], ACT.Copy,
                                   scale=inside[:, ds(n % TS, 1)]).then_inc(shift_r, 1)

                def turned(n, r):
                    g = l * NT + n
                    act.wait_ge(tr_mm, 4 * g + r + 2)
                    if r == 2:
                        act.wait_ge(shift_r, g + 1)
                    dst = (qT[:, 4 * r:4 * r + 4, :] if r < 2 else
                           kT[:, 4 * (r - 2):4 * (r - 2) + 4, WIN:WIN + P])
                    act.activation(dst, c4(ps[:, 2 + r % 2, :]), ACT.Copy).then_inc(tr_ev, 1)

                def exponent(n):
                    g = l * NT + n
                    act.wait_ge(sub_r, g + 1)
                    act.wait_ge(pt_r, g + 1)
                    act.activation(pe_, sc, ACT.Exp).then_inc(exp_r, 1)

                def widen(n, windows):
                    g = l * NT + n
                    if windows[0] == 0:
                        act.wait_ge(pt_r, g + 2)
                        act.wait_ge(pv_mm, 2 * g + 1)
                    for w in windows:
                        q = slice(WIN * w, WIN * (w + 1))
                        i = act.activation(PTd.rearrange("p (k q) -> p k q", q=P)[q, :, q],
                                           pt.rearrange("p (k q) -> p k q", q=WIN)[q, :, :], ACT.Copy)
                    if w == 3:
                        i.then_inc(ptd_r, 1)

                def outputs(n, r):
                    g = l * NT + n
                    act.wait_ge(pv_mm, 2 * g + 1 + r + 1)
                    if r == 0:
                        act.wait_ge(wo_r, g + 1)
                    act.activation(OT[:, 4 * r:4 * r + 4, :], c4(ps[:, 6 + r, :]), ACT.Copy).then_inc(ot_r, 1)

                def values(n, r, c):
                    g = l * NT + n
                    act.wait_ge(v_mm, 2 * g + c + 2)
                    if c == 0:
                        act.wait_ge(vs_in, 32 * g + 1)
                    act.activation(v_[r][:, c * COL:(c + 1) * COL], ps[:, c % 2, :], ACT.Copy)\
                        .then_inc(v_r, 1)

                def step(n, r):
                    if live(n + 1):
                        square(n + 1, 0)
                    if live(n):
                        turned(n, 0)
                        turned(n, 1)
                    if live(n + 1):
                        square(n + 1, 1)
                    if live(n):
                        turned(n, 2)
                        turned(n, 3)
                    if live(n - 1):
                        exponent(n - 1)
                    if live(n - 2):
                        outputs(n - 2, 0)
                    if live(n + 1):
                        square(n + 1, 2)
                        square(n + 1, 3)
                    if live(n - 2):
                        outputs(n - 2, 1)
                    if live(n + 1):
                        values(n + 1, (r + 1) % RING, 0)
                    if live(n - 1):
                        widen(n - 1, (0, 1))
                    if live(n + 1):
                        values(n + 1, (r + 1) % RING, 1)
                    if live(n - 1):
                        widen(n - 1, (2, 3))
                    if live(n + 1):
                        keys_on(n + 1)

                walk(act, step)

                act.wait_ge(y_r, NT * (l + 1) + 1)
                hold(act, lf, 16 * (l + 1))
                with act.Fori(0, NB) as b:
                    v = l * NB + b + 1
                    for u in U:
                        act.wait_ge(LN["nf"]["tr"][u], v)
                        act.activation(tf["xs"][u][0:64, :], Y[0:64, ds(seq_col(b, COL * u), COL)], ACT.Copy)\
                            .then_inc(xlo[u], 1)
                    for u in U:
                        act.wait_ge(LN["nf"]["tb"][u], v)
                        act.activation(tf["xn"][u], ps[:, bank[u][1], :], ACT.Identity,
                                       bias=WF[:, F_B:F_B + 1], scale=WF[:, F_G:F_G + 1]).then_inc(xn_r[u], 1)
                    for m in range(MF):
                        for u in U:
                            act.wait_ge(ag_mm[u], 2 * MF * (v - 1) + 2 * m + 1)
                            act.wait_ge(hf_r[u], MF * (v - 1) + m + 1)
                            act.activation(gf[u][0:FW[m], :], ps[0:FW[m], bank[u][(2 + 2 * m) % 4], :],
                                           ACT.Gelu, bias=WF[0:FW[m], F_BG + m:F_BG + m + 1])\
                                .then_inc(gate_r[u], 1)

        @block.vector
        def _(dve):
            dve.wait_ge(loaded, 64)

            def pre_norm(k):
                with dve.Fori(0, NB) as b:
                    v = k * NB + b + 1
                    for u in U:
                        kc = keep[:, ds(b * SEQ + COL * u, COL)]
                        if k == 0:
                            dve.tensor_copy(ta["z"][u], kc).then_inc(LN["pre"]["z"][u], 1)
                        else:
                            dve.wait_ge(kept[u], b + 1)
                            dve.tensor_tensor(ta["z"][u], kc, X[:, ds(seq_col(b, COL * u), COL)], ALU.add)\
                                .then_inc(LN["pre"]["z"][u], 1)
                    for u in U:
                        ln_stats(dve, "pre", u, v, bank[u][0], EPS_PRE)
                    for u in U:
                        ln_aggr(dve, "pre", u, v, EPS_PRE)
                    for u in U:
                        ln_norm(dve, "pre", u, v, bank[u][0], ta["zn"][u])

            pre_norm(0)
            with dve.Fori(0, BLOCKS) as l:
                dve.wait_ge(la1, 16 * (l + 1))
                dve.tensor_scalar(bias1[:, 0:2], Wa1[:, A1_B:A1_B + 2], 1.0, None, ALU.add).then_inc(biased, 1)
                hold(dve, biased, l + 1)
                with dve.Fori(0, NB) as b:
                    it = l * NB + b
                    for u in U:
                        dve.wait_ge(kvq[u], it + 1)
                        dve.tensor_scalar(ta["mk"][u], ps[:, bank[u][0], :], Wa1[:, A1_B:A1_B + 1], 0.0,
                                          ALU.add, ALU.min).then_inc(mins[u], 1)
                        dve.tensor_scalar(ta["den"][u], ps[:, bank[u][1], :], Wa1[:, A1_B + 1:A1_B + 2], 0.0,
                                          ALU.add, ALU.min).then_inc(mins[u], 1)
                    for u in U:
                        dve.wait_ge(exps[u], 2 * it + 1)
                        dve.scalar_tensor_tensor(ta["K"][u], ps[:, bank[u][0], :], bias1[:, 0:1], ta["ek"][u],
                                                 ALU.add, ALU.max, accum_out=kvp[:, u, 0:1])\
                            .then_inc(k_sum[u], 1)
                        dve.wait_ge(exps[u], 2 * it + 2)
                        dve.tensor_scalar(ta["Vb"][u], ta["Vb"][u], 1.0, 1.0, ALU.subtract, ALU.add)\
                            .then_inc(rounded[u], 1)
                    for u in U:
                        dve.wait_ge(rounded[u], it + 1)
                        dve.scalar_tensor_tensor(Qf[:, ds(b * SEQ + COL * u, COL)], ps[:, bank[u][1], :],
                                                 bias1[:, 1:2], ta["Vb"][u], ALU.add, ALU.max)
                    for u in U:
                        dve.wait_ge(k_sum[u], it + 1)
                        dve.scalar_tensor_tensor(ta["z"][u], ps[:, bank[u][2], :], Wa1[:, A1_B + 2:A1_B + 3],
                                                 ta["K"][u], ALU.add, ALU.mult, accum_out=kvp[:, u, 1:2])\
                            .then_inc(kq_used[u], 1)
                    for u in U:
                        dve.wait_ge(kq_used[u], it + 2)
                    dve.tensor_tensor(kvs[:, ds(b, 1), :], kvp[:, 0:1, :], kvp[:, 1:2, :], ALU.add)\
                        .then_inc(ksum, 1)
                hold(dve, ksum, NB * (l + 1))
                def denominator(t):
                    b, _ = at(t)
                    dve.tensor_scalar(den, Qf[:, q_col(t)], kvs[:, ds(b, 1), 0], EPS_Z, ALU.mult, ALU.add)\
                        .then_inc(vprep, 1)
                    dve.wait_ge(vprep, 3 * upto(l, t) - 2)
                    half = slice(0, COL // 2)
                    dve.reciprocal(recip[:, half], den[:, half]).then_inc(vprep, 1)

                def values(t):
                    b, _ = at(t)
                    v = upto(l, t)
                    half = slice(COL // 2, COL)
                    dve.reciprocal(recip[:, half], den[:, half]).then_inc(vprep, 1)
                    dve.wait_ge(vprep, 3 * v)
                    if not isinstance(t[0], int) or UT * t[0] + t[1] > 0:
                        dve.wait_ge(wo_mm, v - 1)
                    dve.scalar_tensor_tensor(Vb, Qf[:, q_col(t)], kvs[:, ds(b, 1), 1], recip, ALU.mult,
                                             ALU.mult).then_inc(vready, 1)

                def first_sum(t):
                    dve.wait_ge(ga, upto(l, t))
                    dve.tensor_tensor(z1, g1, X[:, x_col(t)], ALU.add).then_inc(LN["n1"]["z"][0], 1)

                def second_sum(t):
                    dve.wait_ge(g2_r, upto(l, t))
                    dve.tensor_tensor(z2, g2, x1[at(t)[1]], ALU.add).then_inc(LN["n2"]["z"][1], 1)

                def step(t):
                    if has(by(t, 1)):
                        v = upto(l, by(t, 1))
                        ln_stats(dve, "n1", 0, v, TURN_BANK[0], EPS_A)
                        ln_aggr(dve, "n1", 0, v, EPS_A)
                    if has(by(t, -1)):
                        second_sum(by(t, -1))
                    if has(by(t, 1)):
                        ln_norm(dve, "n1", 0, v, TURN_BANK[0], zn1)
                    if has(by(t, -1)):
                        w = upto(l, by(t, -1))
                        ln_stats(dve, "n2", 1, w, TURN_BANK[1], EPS_A)
                        ln_aggr(dve, "n2", 1, w, EPS_A)
                        dve.tensor_scalar(mneg[:, :], mv[:, 1, :, 0], -1.0, None, ALU.mult).then_inc(mneg_r, 1)
                    if has(by(t, 3)):
                        denominator(by(t, 3))
                    if has(by(t, 2)):
                        first_sum(by(t, 2))
                    if has(by(t, 3)):
                        values(by(t, 3))

                march(dve, step)
            for u in U:
                dve.wait_ge(x_done[u], NB * (BLOCKS + 1) + 1)
            pre_norm(1)

            dve.wait_ge(consts, 8)
            with dve.Fori(0, LAYERS) as l:
                for u in U:
                    dve.wait_ge(x_done[u], NB * (BLOCKS + 2 + l) + 1)
                dve.wait_ge(lb, 16 * (l + 1))
                for i in range(4):
                    s = WB[:, B_SC + i * DH:B_SC + (i + 1) * DH].unsqueeze(1).to_broadcast([P, TS, DH])
                    dve.tensor_tensor(tables[:, i, :, :], rotary[:, i, :, :], s, ALU.mult).then_inc(tab_r, 1)
                dve.wait_ge(tab_r, 4 * (l + 1))

                def xs(n, r, half):
                    g = l * NT + n
                    c = tile_col(n)
                    if not isinstance(n, int) or n >= RING:
                        dve.wait_ge(v_mm, 2 * (g - RING) + 3)
                    dve.tensor_copy(xs_[r][64 * half:64 * half + 64, :],
                                    X[64 * half:64 * half + 64, ds(c - half, P)]).then_inc(xs_r, 1)

                def rotate(n, c):
                    g = l * NT + n
                    hc = COL // DH
                    dve.wait_ge(sq_r, QKC * g + c + 1)
                    if c == 0:
                        dve.wait_ge(tr_mm, 4 * g + 1)
                    o = 2 * (c // 2)
                    src = ps[:, c % 2, :].rearrange("p (h d) -> p h d", d=DH)
                    a = t1[:, c * COL:(c + 1) * COL].rearrange("p (h d) -> p h d", d=DH)
                    bdst = t2[:, c * COL:(c + 1) * COL].rearrange("p (h d) -> p h d", d=DH)
                    cos = tables[:, o, ds(n % TS, 1), :].to_broadcast([P, hc, DH])
                    dve.tensor_tensor(a, src, cos, ALU.mult)
                    if c == 0:
                        dve.wait_ge(add_r, QKC * g + 1)
                    for i in range(2):
                        here, there = slice(32 * i, 32 * i + 32), slice(32 - 32 * i, 64 - 32 * i)
                        sin = tables[:, o + 1, ds(n % TS, 1), here].to_broadcast([P, hc, 32])
                        k = dve.tensor_tensor(bdst[:, :, here], src[:, :, there], sin, ALU.mult)
                    k.then_inc(rot_r, 1)

                def sumsq(n, c):
                    dve.tensor_reduce(ssq[:, 8 * c:8 * c + 8],
                                      sq[:, c * COL:(c + 1) * COL].rearrange("p (h d) -> p h d", d=DH),
                                      AX_X, ALU.add).then_inc(red_r, 1)

                def clamp(n):
                    g = l * NT + n
                    dve.wait_ge(red_r, QKC * (g + 1) + 1)
                    dve.tensor_scalar(ssc[:, :], ssq[:, :], NORM_MIN, None, ALU.max).then_inc(ssc_r, 1)

                def roots(n, between):
                    g = l * NT + n
                    k = (3 * NEWTON + 1) * g
                    dve.wait_ge(ssc_r, g + 1)
                    if not isinstance(n, int) or n > 0:
                        dve.wait_ge(k_r, g)
                    dve.tensor_scalar(rinv[:, :].bitcast(I32), ssc[:, :].bitcast(I32), -0.5, ROOT_BITS,
                                      ALU.mult, ALU.add).then_inc(newton, 1)
                    for i in range(NEWTON):
                        if between and i < 2:
                            between(i)
                        dve.wait_ge(newton, k + 3 * i + 1)
                        dve.scalar_tensor_tensor(nwt[:, 0, :], rinv[:, :], -0.5, rinv[:, :], ALU.mult,
                                                 ALU.mult).then_inc(newton, 1)
                        dve.wait_ge(newton, k + 3 * i + 2)
                        dve.tensor_tensor(nwt[:, 1, :], nwt[:, 0, :], ssc[:, :], ALU.mult).then_inc(newton, 1)
                        dve.wait_ge(newton, k + 3 * i + 3)
                        dve.scalar_tensor_tensor(rinv[:, :], nwt[:, 1, :], 1.5, rinv[:, :], ALU.add,
                                                 ALU.mult).then_inc(newton, 1)

                def unit(n):
                    g = l * NT + n
                    dve.wait_ge(newton, (3 * NEWTON + 1) * (g + 1))
                    dve.wait_ge(add_r, QKC * (g + 1) + 1)
                    t3 = heads(t1)[:, 0:HEADS, :]
                    dve.tensor_tensor(t3, t3, rinv[:, 0:HEADS].unsqueeze(2).to_broadcast([P, HEADS, DH]),
                                      ALU.mult).then_inc(q_r, 1)

                def masked(n):
                    g = l * NT + n
                    dve.wait_ge(s_mm, g + 2)
                    for a in range(2):
                        m = maskt[:, ds(n % TS, 1), :].to_broadcast([P, NP, 2 * WIN])
                        i = dve.tensor_tensor(sc.rearrange("p (a h k) -> p a h k", a=2, h=NP)[:, a],
                                              ps[:, 4 + a, :].rearrange("p (h k) -> p h k", h=NP), m, ALU.add)
                    i.then_inc(s_rd, 1)
                    dve.wait_ge(s_rd, g + 2)
                    dve.tensor_reduce(mx[:, :], sc.rearrange("p (h k) -> p h k", h=HEADS), AX_X, ALU.max)\
                        .then_inc(max_r, 1)

                def totals(n):
                    g = l * NT + n
                    dve.wait_ge(exp_r, g + 1)
                    dve.tensor_reduce(rs[:, :], pe_.rearrange("p (h k) -> p h k", h=HEADS), AX_X, ALU.add)\
                        .then_inc(sum_r, 1)
                    dve.wait_ge(sum_r, g + 1)
                    dve.reciprocal(rr[:, :], rs[:, :]).then_inc(rec_r, 1)

                def turn_probs(n):
                    g = l * NT + n
                    dve.wait_ge(p_r, g + 1)
                    dve.wait_ge(ptd_r, g + 1)
                    dve.transpose(pt, pe_).then_inc(pt_r, 1)

                def residual(n):
                    g = l * NT + n
                    c = tile_col(n)
                    dve.wait_ge(wo_r, g + 2)
                    dve.tensor_tensor(Y[:, ds(c, P)], ps[:, 6, 0:P], X[:, ds(c, P)], ALU.add).then_inc(y_r, 1)

                def step(n, r):
                    if not live(n + 1) and live(n + 2):
                        for i in range(2):
                            xs(n + 2, (r + 2) % RING, i)
                    if live(n - 1):
                        masked(n - 1)
                    if live(n - 3):
                        residual(n - 3)
                    if live(n + 1):
                        for c in (0, 1):
                            rotate(n + 1, c)
                            sumsq(n + 1, c)
                    if live(n - 1):
                        totals(n - 1)
                    if live(n + 1):
                        rotate(n + 1, 2)
                        sumsq(n + 1, 2)
                        rotate(n + 1, 3)
                    if live(n - 1):
                        turn_probs(n - 1)
                    if live(n + 1):
                        sumsq(n + 1, 3)
                        clamp(n + 1)
                        after = (lambda half: xs(n + 2, (r + 2) % RING, half)) if live(n + 2) else None
                        roots(n + 1, after)
                        unit(n + 1)

                walk(dve, step)

                dve.wait_ge(lf, 16 * (l + 1))
                hold(dve, y_r, NT * (l + 1) + 1)
                with dve.Fori(0, NB) as b:
                    v = l * NB + b + 1
                    for u in U:
                        dve.wait_ge(LN["nf"]["tr"][u], v)
                        dve.tensor_copy(tf["xs"][u][64:P, :], Y[64:P, ds(seq_col(b, COL * u) - 1, COL)])\
                            .then_inc(xhi[u], 1)
                    for u in U:
                        ln_stats(dve, "nf", u, v, bank[u][0], EPS_F)
                    for u in U:
                        ln_aggr(dve, "nf", u, v, EPS_F)
                    for u in U:
                        ln_norm(dve, "nf", u, v, bank[u][0], tf["zn"][u])
                    for m in range(MF):
                        for u in U:
                            dve.wait_ge(gate_r[u], MF * (v - 1) + m + 1)
                            dve.wait_ge(ag_mm[u], 2 * MF * (v - 1) + 2 * m + 2)
                            dve.scalar_tensor_tensor(hf[u][0:FW[m], m, :],
                                                     ps[0:FW[m], bank[u][(3 + 2 * m) % 4], :],
                                                     WF[0:FW[m], F_BA + m:F_BA + m + 1], gf[u][0:FW[m], :],
                                                     ALU.add, ALU.mult).then_inc(hf_r[u], 1)
                    for u in U:
                        col = ds(seq_col(b, COL * u), COL)
                        dve.wait_ge(o_mm[u], v)
                        dve.scalar_tensor_tensor(X[:, col], ps[:, bank[u][0], :], WF[:, F_B2:F_B2 + 1],
                                                 Y[:, col], ALU.add, ALU.add).then_inc(x_done[u], 1)
            for u in U:
                dve.wait_ge(x_done[u], NB * (BLOCKS + 2 + LAYERS) + 1)
            with dve.Fori(0, NB) as b:
                dve.tensor_tensor(keep[:, ds(b * SEQ, SEQ)], keep[:, ds(b * SEQ, SEQ)],
                                  X[:, ds(seq_col(b, 0), SEQ)], ALU.add).then_inc(finals, 1)


def constant_tables():
    f = np.float32
    half = np.arange(0, DH, 2, dtype=f)
    inv = (f(1.0) / f(10000.0) ** (half / f(DH))).astype(f)
    t = np.arange(SEQ, dtype=f)
    fr = t[:, None] * inv[None, :]
    fr = np.concatenate([fr, fr], -1).astype(np.float64)
    base = ((half + f(0.4 * DH)) / f(1.4 * DH)).astype(f)
    power = (t - SEQ // 2) / (WIN // 2)
    scale = base[None, :].astype(np.float64) ** power[:, None]
    scale = np.concatenate([scale, scale], -1)
    sign = np.concatenate([-np.ones(DH // 2), np.ones(DH // 2)])
    cos, sin = np.cos(fr), np.sin(fr) * sign
    rot = np.stack([QK_SCALE * cos * scale, QK_SCALE * sin * scale, cos / scale, sin / scale]).astype(f)
    rot = rot.reshape(4, TS, P, DH).transpose(2, 0, 1, 3).reshape(P, 4 * TS * DH)
    i, j = np.arange(WIN)[:, None], np.arange(WIN)[None, :]
    before, own = np.where(i > j, NEG, 0.0), np.where(i < j, NEG, 0.0)
    mask = np.tile(np.concatenate([before, own], 1)[None, None], (TS, P // WIN, 1, 1))
    mask[0, 0, :, :WIN] = NEG
    mask = mask.reshape(TS, P, 2 * WIN).transpose(1, 0, 2).reshape(P, TS * 2 * WIN).astype(f)
    mask = np.concatenate([mask, np.tile((np.arange(TS) > 0).astype(f), (P, 1))], 1)
    return np.ascontiguousarray(rot), np.ascontiguousarray(mask)


def kernel(**inputs):
    import concourse.bacc as _bacc
    from concourse.bass_utils import run_bass_kernel_spmd as _run

    i = {k: np.asarray(v) for k, v in inputs.items()}
    A = {k[len("L0_attn_"):]: v for k, v in i.items() if k.startswith("L0_attn_")}
    B = {k[len("L0_ffn_"):]: v for k, v in i.items() if k.startswith("L0_ffn_")}

    def col(v):
        return v[:, :, None]

    def chunks(w, n, rows):
        full = np.zeros((w.shape[0], n * P, w.shape[2]), w.dtype)
        full[:, :rows] = w
        return full.reshape(w.shape[0], n, P, -1).transpose(0, 2, 1, 3).reshape(w.shape[0], P, -1)

    wa1 = np.concatenate([A["Wq"], A["Wk"], A["Wv"], col(A["bk"]), col(A["bq"]), col(A["bv"])], 2)
    wa2 = np.concatenate([A["Wo"], A["Wf1"], chunks(A["Wf2"], MA, FA), col(A["bo"]), col(A["ln1_s"]),
                          col(A["ln1_b"]), chunks(col(A["bf1"]), MA, FA), col(A["bf2"]), col(A["ln2_s"]),
                          col(A["ln2_b"])], 2)

    def spread(v):
        return np.broadcast_to(v[:, None, :], (LAYERS, P, DH))

    def swap(v):
        return np.concatenate([v[:, DH // 2:], v[:, :DH // 2]], 1)

    qs, ks = B["q_scale"], B["k_scale"]
    wb = np.concatenate([B["Wqkv"], chunks(B["Wo"], NP, INNER), spread(qs), spread(swap(qs)), spread(ks),
                         spread(swap(ks))], 2)
    wf = np.concatenate([B["W1"], chunks(B["W2"], MF, HID), col(B["ln_g"]), col(B["ln_b"]),
                         chunks(col(B["b1"][:, :HID]), MF, HID), chunks(col(B["b1"][:, HID:]), MF, HID),
                         col(B["b2"])], 2)
    rot, mask = constant_tables()
    arrays = {"xT": A["x"].reshape(NB * SEQ, D).T, "wa1": wa1.reshape(-1, A1_W), "wa2": wa2.reshape(-1, A2_W),
              "wb": wb.reshape(-1, B_W), "wf": wf.reshape(-1, F_W), "rot": rot, "mask": mask}
    arrays = {k: np.ascontiguousarray(v) for k, v in arrays.items()}
    nc = _bacc.Bacc("TRN2", target_bir_lowering=False, num_devices=1)
    args = [nc.dram_tensor(k, v.shape, F32, kind="ExternalInput").ap() for k, v in arrays.items()]
    out = nc.dram_tensor("outT", [D, NB * SEQ], F32, kind="ExternalOutput").ap()
    build(nc, *args, out)
    r = _run(nc, [arrays], core_ids=[0])
    return np.ascontiguousarray(r.results[0]["outT"].T).reshape(NB, SEQ, D)
```
